# Optimizing a Trainium2 kernel written in Bass

```python
import numpy as np
import jax
import jax.numpy as jnp

def _softmax(x, axis=-1):
    return jax.nn.softmax(x, axis=axis)

def _gelu(x):
    return jax.nn.gelu(x, approximate=True)

def _silu(x):
    return jax.nn.silu(x)

def _sigmoid(x):
    return jax.nn.sigmoid(x)

def _layernorm(x, axis=-1, eps=1e-05):
    m = jnp.mean(x, axis=axis, keepdims=True)
    v = jnp.var(x, axis=axis, keepdims=True)
    return (x - m) / jnp.sqrt(v + eps)

def _scatter_add(tgt, idx, src, axis=0):
    return tgt.at[idx].add(src)

def _segment_sum(src, seg, n):
    return jax.ops.segment_sum(src, seg, n)
kernel_name = 'mk_flamingo_gated_d1_seqx_r8_8a1ce5'

def setup_inputs(seed: int=0):
    np.random.seed(seed)
    _w = jnp.asarray

    def _rec_inputs():
        import jax
        import jax.numpy as jnp
        _rk = jax.random.key(seed)
        x = -0.0002928 + 1 * jax.random.normal(jax.random.fold_in(_rk, 1), (128, 64, 128), jnp.float32)
        _lenS = 64 - jax.random.randint(jax.random.fold_in(_rk, 7), (128,), 0, max(1, 64 // 4) + 1, jnp.int32)
        _lenS2 = 64 - jax.random.randint(jax.random.fold_in(_rk, 8), (128,), 0, max(1, 64 // 4) + 1, jnp.int32)
        _ctx_1024P = jax.random.normal(jax.random.fold_in(_rk, 11), (128, 16, 128), jnp.float32)
        _ctx_1024c = jax.random.dirichlet(jax.random.fold_in(_rk, 511), 0.3 * jnp.ones((16,), jnp.float32), (128, 64))
        _ctx_1024t = jnp.einsum('bsk,bkd->bsd', _ctx_1024c, _ctx_1024P)
        _ctx_1024t = _ctx_1024t * jax.lax.rsqrt(jnp.mean(jnp.square(_ctx_1024t)) + 1e-12) * 0.953939
        ctx_1024 = -1.39393e-06 + 0.999914 * (_ctx_1024t + 0.3 * jax.random.normal(jax.random.fold_in(_rk, 611), (128, 64, 128), jnp.float32))
        _g = jax.random.normal(jax.random.fold_in(_rk, 9001), (2, 1), jnp.float32)
        _g = jnp.sign(_g) * jnp.maximum(jnp.abs(_g), 1.0) + (_g == 0) * 1.0
        g_xattn = _g[0]
        g_ffn = _g[1]
        return (x, ctx_1024, g_xattn, g_ffn)
    x, ctx_1024, g_xattn, g_ffn = _rec_inputs()

    def _L0_xattn_setup():
        import jax, jax.numpy as jnp
        import numpy as np
        D_MODEL = 128
        N_HEADS = 16
        BATCH = 2
        SEQ = 256

        def _rope(x):
            d = x.shape[-1]
            half = d // 2
            seq = x.shape[-2]
            pos = jnp.arange(seq, dtype=jnp.float32)
            theta = 1.0 / 10000.0 ** (2.0 * jnp.arange(half, dtype=jnp.float32) / d)
            ang = pos[:, None] * theta[None, :]
            sin, cos = (jnp.sin(ang), jnp.cos(ang))
            x1 = x[..., 0::2]
            x2 = x[..., 1::2]
            r1 = x1 * cos - x2 * sin
            r2 = x1 * sin + x2 * cos
            return jnp.stack([r1, r2], axis=-1).reshape(x.shape)
        key = jax.random.key(seed)
        ks = jax.random.split(key, 8)
        s = 1.0 / np.sqrt(D_MODEL)
        return {'q': jax.random.normal(ks[0], (BATCH, SEQ, D_MODEL), jnp.float32), 'k': jax.random.normal(ks[1], (BATCH, SEQ, D_MODEL), jnp.float32), 'v': jax.random.normal(ks[2], (BATCH, SEQ, D_MODEL), jnp.float32), 'Wq': jax.random.normal(ks[3], (D_MODEL, D_MODEL), jnp.float32) * s, 'Wk': jax.random.normal(ks[4], (D_MODEL, D_MODEL), jnp.float32) * s, 'Wv': jax.random.normal(ks[5], (D_MODEL, D_MODEL), jnp.float32) * s, 'Wp': jax.random.normal(ks[6], (D_MODEL, D_MODEL), jnp.float32) * s, 'bp': jax.random.normal(ks[7], (D_MODEL,), jnp.float32) * s}
    _L0_xattn_all = _L0_xattn_setup()
    _L0_xattn_in = {k: v for k, v in _L0_xattn_all.items() if k in ('Wq', 'Wk', 'Wv', 'Wp', 'bp')}
    del _L0_xattn_all

    def _L0_ffn_setup():
        import jax, jax.numpy as jnp
        import numpy as np
        NUM_EXPERTS = 8
        TOP_K = 2
        key = jax.random.key(seed)
        ks = jax.random.split(key, 5)
        B, L, E, H, N = (2, 256, 128, 256, NUM_EXPERTS)
        return {'x': jax.random.normal(ks[0], (B, L, E), dtype=jnp.float32), 'gate_kernel': jax.random.normal(ks[1], (E, N), dtype=jnp.float32) / np.sqrt(E), 'w0_kernel': jax.random.normal(ks[2], (N, E, H), dtype=jnp.float32) / np.sqrt(E), 'w1_kernel': jax.random.normal(ks[3], (N, E, H), dtype=jnp.float32) / np.sqrt(E), 'wo_kernel': jax.random.normal(ks[4], (N, H, E), dtype=jnp.float32) / np.sqrt(H)}
    _L0_ffn_all = _L0_ffn_setup()
    _L0_ffn_in = {k: v for k, v in _L0_ffn_all.items() if k in ('gate_kernel', 'w0_kernel', 'w1_kernel', 'wo_kernel')}
    del _L0_ffn_all
    return {'x': x, 'ctx_1024': ctx_1024, 'g_xattn': g_xattn, 'g_ffn': g_ffn, 'L0_xattn_Wq': _L0_xattn_in['Wq'], 'L0_xattn_Wk': _L0_xattn_in['Wk'], 'L0_xattn_Wv': _L0_xattn_in['Wv'], 'L0_xattn_Wp': _L0_xattn_in['Wp'], 'L0_xattn_bp': _L0_xattn_in['bp'], 'L0_ffn_gate_kernel': _L0_ffn_in['gate_kernel'], 'L0_ffn_w0_kernel': _L0_ffn_in['w0_kernel'], 'L0_ffn_w1_kernel': _L0_ffn_in['w1_kernel'], 'L0_ffn_wo_kernel': _L0_ffn_in['wo_kernel']}

def reference(x, ctx_1024, g_xattn, g_ffn, L0_xattn_Wq, L0_xattn_Wk, L0_xattn_Wv, L0_xattn_Wp, L0_xattn_bp, L0_ffn_gate_kernel, L0_ffn_w0_kernel, L0_ffn_w1_kernel, L0_ffn_wo_kernel):
    import jax
    import jax.numpy as jnp

    def _L0_xattn_ref(q, k, v, Wq, Wk, Wv, Wp, bp):
        import jax, jax.numpy as jnp
        import numpy as np
        D_MODEL = 128
        N_HEADS = 16
        BATCH = 2
        SEQ = 256

        def _rope(x):
            d = x.shape[-1]
            half = d // 2
            seq = x.shape[-2]
            pos = jnp.arange(seq, dtype=jnp.float32)
            theta = 1.0 / 10000.0 ** (2.0 * jnp.arange(half, dtype=jnp.float32) / d)
            ang = pos[:, None] * theta[None, :]
            sin, cos = (jnp.sin(ang), jnp.cos(ang))
            x1 = x[..., 0::2]
            x2 = x[..., 1::2]
            r1 = x1 * cos - x2 * sin
            r2 = x1 * sin + x2 * cos
            return jnp.stack([r1, r2], axis=-1).reshape(x.shape)
        h = N_HEADS
        b, s, d = q.shape
        dh = d // h
        qp = q @ Wq.T
        kp = k @ Wk.T
        vp = v @ Wv.T
        kp = _rope(kp)
        vp = _rope(vp)
        qh = qp.reshape(b, s, h, dh).transpose(0, 2, 1, 3)
        kh = kp.reshape(b, s, h, dh).transpose(0, 2, 1, 3)
        vh = vp.reshape(b, s, h, dh).transpose(0, 2, 1, 3)
        scores = jnp.einsum('bhqd,bhkd->bhqk', qh, kh) / jnp.sqrt(jnp.float32(dh))
        weights = jax.nn.softmax(scores, axis=-1)
        ctx = jnp.einsum('bhqk,bhkd->bhqd', weights, vh)
        ctx = ctx.transpose(0, 2, 1, 3).reshape(b, s, d)
        return ctx @ Wp.T + bp

    def _L0_ffn_ref(x, gate_kernel, w0_kernel, w1_kernel, wo_kernel):
        import jax, jax.numpy as jnp
        import numpy as np
        NUM_EXPERTS = 8
        TOP_K = 2
        B, L, E = x.shape
        gate_logits = jnp.einsum('ble,en->bln', x, gate_kernel)
        top_k_weights, top_k_indices = jax.lax.top_k(gate_logits, TOP_K)
        softmax_probs = jax.nn.softmax(top_k_weights.astype(jnp.float32), axis=-1)
        weights = jnp.zeros_like(gate_logits)
        b_idx = jnp.arange(B)[:, None, None]
        l_idx = jnp.arange(L)[:, None]
        weights = weights.at[b_idx, l_idx, top_k_indices].set(softmax_probs)
        layer_w0 = jnp.einsum('ble,neh->blnh', x, w0_kernel)
        layer_w1 = jnp.einsum('ble,neh->blnh', x, w1_kernel)
        layer_mult = jax.nn.silu(layer_w0) * layer_w1
        intermediate = jnp.einsum('blnh,nhe->blne', layer_mult, wo_kernel)
        output = jnp.einsum('blne,bln->ble', intermediate, weights)
        return output
    x = x + jnp.tanh(g_xattn[0]) * _L0_xattn_ref(_layernorm(x, axis=-1), ctx_1024, ctx_1024, L0_xattn_Wq, L0_xattn_Wk, L0_xattn_Wv, L0_xattn_Wp, L0_xattn_bp)
    x = x + jnp.tanh(g_ffn[0]) * _L0_ffn_ref(_layernorm(x, axis=-1), L0_ffn_gate_kernel, L0_ffn_w0_kernel, L0_ffn_w1_kernel, L0_ffn_wo_kernel)
    return x

_drawn_inputs = setup_inputs


def setup_inputs(seed=0):
    import zlib

    import numpy as np

    out = dict(_drawn_inputs(seed))
    spreads = {}
    factors = {}
    for name, (base, spread) in spreads.items():
        noise = np.random.default_rng([zlib.crc32(name.encode()), seed]).standard_normal(out[name].shape)
        drawn = base * np.exp(spread * noise) if base else spread * noise
        out[name] = jnp.asarray(drawn.astype(out[name].dtype))
    for name, factor in factors.items():
        out[name] = (out[name] * factor).astype(out[name].dtype)
    return out
```

```python
from contextlib import ExitStack

import concourse.bass as bass
from concourse import mybir

F32 = mybir.dt.float32
U32 = mybir.dt.uint32
ALU = mybir.AluOpType
ACT = mybir.ActivationFunctionType
AX_X = mybir.AxisListType.X

P = 128
NB, S, D = 128, 64, 128
H, DH = 16, 8
NT = NB * S // P
PAIRS = H // 2
E, HID = 8, 256
EPS = 1e-5
SCALE = float(DH) ** -0.5
VW = 2 * (DH + 1)
VPAD = 64
VROW = (PAIRS - 1) * VW + VPAD
OROW = 192
FIRST, LAST = -4, NT + 1
STEADY = 5
TURNS = (NT - 4 - STEADY) // 4


class Tile:

    def __init__(self, val, mod):
        self.val, self.mod = val, mod

    def buf(self, n):
        return self.mod % n

    def __add__(self, n):
        return Tile(self.val + n, self.mod + n)


def at_step(step, off):
    turn, u = step
    if turn is None:
        return Tile(u + off, u + off) if 0 <= u + off < NT else None
    return Tile(4 * turn + (STEADY + u + off), STEADY + u + off)


def pipeline(eng, body):
    for t in range(FIRST, STEADY):
        body((None, t))
    with eng.Fori(0, TURNS) as turn:
        for u in range(4):
            body((turn, u))
    for t in range(STEADY + 4 * TURNS, LAST + 1):
        body((None, t))


def wait_for(eng, sem, t, back=0, per=1, part=None):
    v = per * (t.val - back) + (per if part is None else part + 1)
    if isinstance(v, int) and v <= 0:
        return
    eng.wait_ge(sem, v)


def carry(eng):
    eng.nop(nofuse=True)


def flamingo_block(nc, A, out):
    with ExitStack() as ctx:
        def sb(name, shape, dt=F32):
            return ctx.enter_context(nc.sbuf_tensor(name, shape, dt))

        def ps(name):
            return ctx.enter_context(nc.psum_tensor(name, [P, 512], F32))

        def sem(name):
            return ctx.enter_context(nc.semaphore(name))

        xres = sb("xres", [P, NT, D])
        cring = sb("cring", [P, 4, D])
        zT = sb("zT", [P, NT, P])
        ident = sb("ident", [P, P])
        wnat = sb("wnat", [P, 4, D])
        wT = sb("wT", [P, 4, D])
        wperm = sb("wperm", [P, D])
        cosT = sb("cosT", [P, D])
        sinT = sb("sinT", [P, D])
        hmask = sb("hmask", [P, 4])
        gcol = sb("gcol", [P, 2])
        tg = sb("tg", [P, 2])
        bp = sb("bp", [P, D])
        bpg = sb("bpg", [P, D])
        mhalf = sb("mhalf", [P, 1])
        gatew = sb("gatew", [P, D])
        w0 = sb("w0", [P, E, HID])
        w1 = sb("w1", [P, E, HID])
        wo = sb("wo", [P, E, 2, D])
        st1, st2 = sb("st1", [P, 2, 6]), sb("st2", [P, 2, 6])
        mv1, mv2 = sb("mv1", [P, 2, 2]), sb("mv2", [P, 2, 2])
        ve1, ve2 = sb("ve1", [P, 2, 1]), sb("ve2", [P, 2, 1])
        rs1, rs2 = sb("rs1", [P, 2, 1]), sb("rs2", [P, 2, 1])
        xn = sb("xn", [P, 2, D])
        xcT = sb("xcT", [P, 2, 2 * D])
        ropA = sb("ropA", [P, 2, 2 * D])
        ropB = sb("ropB", [P, 2, 2 * D])
        kr = sb("kr", [P, 2, D])
        qblk = sb("qblk", [P, 2, 2, 4, S])
        kfull = sb("kfull", [P, 2, 4, D])
        v9 = sb("v9", [P, 4, 2, VROW])
        sx = sb("sx", [P, 2, 512])
        ex = sb("ex", [P, 2, 2, 512])
        mx = sb("mx", [P, 2, PAIRS])
        pT = sb("pT", [P, 2, 2, 512])
        rden = sb("rden", [S, 2, 2 * PAIRS])
        on = sb("on", [P, 2, D])
        oT = sb("oT", [P, 2, D])
        zn = sb("zn", [P, 2, D])
        zTs = sb("zTs", [P, 2, D])
        lg = sb("lg", [P, NT, E])

        psS = [ps("psS0"), ps("psS1")]
        psP = [ps("psP0"), ps("psP1")]
        psX = ps("psX")
        psK = ps("psK")
        psO = ps("psO")
        psG = ps("psG")

        weights_in, experts_in, tiles_in = sem("weights_in"), sem("experts_in"), sem("tiles_in")
        ident_ready, zero_ready, ones_ready = sem("ident_ready"), sem("zero_ready"), sem("ones_ready")
        wp_ready = sem("wp_ready")
        wT_ps, wT_sb, tanh_ready, bias_ready, half_ready = sem("wT_ps"), sem("wT_sb"), sem("tanh_ready"), sem("bias_ready"), sem("half_ready")
        st1_done, mv1_done, ve1_done, rs1_done = sem("st1_done"), sem("mv1_done"), sem("ve1_done"), sem("rs1_done")
        xn_done, xb_done, xc_ps, xc_sb = sem("xn_done"), sem("xb_done"), sem("xc_ps"), sem("xc_sb")
        q_ps, kv_ps, q_sb, rope_done = sem("q_ps"), sem("kv_ps"), sem("q_sb"), sem("rope_done")
        kr_done, v9_done, kT_ps, kT_sb = sem("kr_done"), sem("v9_done"), sem("kT_ps"), sem("kT_sb")
        s_ps, mx_done, sub_done, exp_done = sem("s_ps"), sem("mx_done"), sem("sub_done"), sem("exp_done")
        p_ps, p_sb, pv_ps, rden_done, on_done = sem("p_ps"), sem("p_sb"), sem("pv_ps"), sem("rden_done"), sem("on_done")
        oT_ps, oT_sb, attn_ps, x1_done = sem("oT_ps"), sem("oT_sb"), sem("attn_ps"), sem("x1_done")
        st2_done, mv2_done, ve2_done, rs2_done = sem("st2_done"), sem("mv2_done"), sem("ve2_done"), sem("rs2_done")
        zn_done, z_ps, z_sb, lg_ps, lg_sb = sem("zn_done"), sem("z_ps"), sem("z_sb"), sem("lg_ps"), sem("lg_sb")

        x_d = A["x"].rearrange("b s d -> (b s) d").rearrange("(t p) d -> p t d", p=P)
        c_d = A["ctx_1024"].rearrange("b s d -> (b s) d").rearrange("(t p) d -> p t d", p=P)
        o_d = out.rearrange("b s d -> (b s) d").rearrange("(t p) d -> p t d", p=P)

        def one(ap, t):
            return ap[:, t.val, :] if isinstance(t.val, int) else ap[:, bass.ds(t.val, 1), :].squeeze(1)

        with nc.Block() as block:
            @block.sync
            def _(sp):
                for n, w in enumerate(("L0_xattn_Wq", "L0_xattn_Wk", "L0_xattn_Wv", "L0_xattn_Wp")):
                    sp.dma_start(wnat[:, n, :], A[w]).then_inc(weights_in, 16)
                sp.dma_start(cosT[:, :], A["rope_cos"]).then_inc(weights_in, 16)
                sp.dma_start(sinT[:, :], A["rope_sin"]).then_inc(weights_in, 16)
                sp.dma_start(hmask[:, :], A["head_mask"]).then_inc(weights_in, 16)
                sp.dma_start(gcol[:, 0:1], A["g_xattn"].unsqueeze(0).broadcast_to([P, 1])).then_inc(weights_in, 16)
                sp.dma_start(gcol[:, 1:2], A["g_ffn"].unsqueeze(0).broadcast_to([P, 1])).then_inc(weights_in, 16)
                sp.dma_start(bp[:, :], A["L0_xattn_bp"].unsqueeze(0).broadcast_to([P, D])).then_inc(weights_in, 16)
                sp.wait_ge(zero_ready, 4)
                sp.dma_start(gatew[:, 0:E], A["L0_ffn_gate_kernel"]).then_inc(weights_in, 16)

                def load(t):
                    wait_for(sp, tiles_in, t, back=1, per=32)
                    carry(sp)
                    wait_for(sp, xc_ps, t, back=4)
                    carry(sp)
                    sp.dma_start(one(xres, t), one(x_d, t)).then_inc(tiles_in, 16)
                    sp.dma_start(cring[:, t.buf(4), :], one(c_d, t)).then_inc(tiles_in, 16)

                for t in range(4):
                    load(Tile(t, t))
                with sp.Fori(1, NT // 4) as turn:
                    for u in range(4):
                        load(Tile(4 * turn + u, u))
                sp.dma_start(w0[:, :, :], A["L0_ffn_w0_kernel"].rearrange("e d h -> d e h")).then_inc(experts_in, 16)
                sp.dma_start(w1[:, :, :], A["L0_ffn_w1_kernel"].rearrange("e d h -> d e h")).then_inc(experts_in, 16)
                for e in range(E):
                    sp.dma_start(wo[:, e, :, :], A["L0_ffn_wo_kernel"][e].rearrange("(k h) d -> h k d", k=2)).then_inc(experts_in, 16)

            @block.tensor
            def _(pe):
                pe.wait_ge(weights_in, 16 * 11)
                pe.wait_ge(ident_ready, 2)
                pe.wait_ge(wp_ready, 2)
                for n in range(4):
                    last = pe.transpose(psS[0][:, n * D:(n + 1) * D], wnat[:, n, :] if n < 3 else wperm[:, :], ident[:, :])
                last.then_inc(wT_ps, 1)
                pe.wait_ge(wT_sb, 2)
                pe.wait_ge(ones_ready, 1)

                def step(s):
                    if t := at_step(s, 1):
                        wait_for(pe, kT_sb, t)
                        wait_for(pe, q_sb, t)
                        for b in range(2):
                            wait_for(pe, sub_done, t, back=1, per=2, part=b)
                            for jp in range(2):
                                last = pe.matmul(psS[b][:, jp * 256:(jp + 1) * 256],
                                                 qblk[:, t.buf(2), b, 2 * jp:2 * jp + 2, :].rearrange("p j q -> p (j q)"),
                                                 kfull[:, t.buf(2), :, b * S:(b + 1) * S], start=True, stop=True)
                            last.then_inc(s_ps, 1)
                    if t := at_step(s, -1):
                        wait_for(pe, oT_sb, t)
                        wait_for(pe, lg_sb, t, back=1)
                        pe.matmul(psG[:, 0:D], oT[:, t.buf(2), :], wT[:, 3, :], start=True, stop=True).then_inc(attn_ps, 1)
                    if t := at_step(s, 0):
                        for b in range(2):
                            wait_for(pe, exp_done, t, per=2, part=b)
                            wait_for(pe, p_sb, t, back=1, per=2, part=b)
                            for n in range(4):
                                last = pe.transpose(psP[b][:, n * P:(n + 1) * P],
                                                    ex[:, t.buf(2), b, n * P:(n + 1) * P], ident[:, :])
                            last.then_inc(p_ps, 1)
                    if t := at_step(s, 2):
                        wait_for(pe, kr_done, t)
                        pe.transpose(psK[:, 256:384], kr[:, t.buf(2), :], ident[:, :]).then_inc(kT_ps, 1)
                    if t := at_step(s, 3):
                        wait_for(pe, xn_done, t)
                        wait_for(pe, tiles_in, t, per=32)
                        wait_for(pe, q_sb, t, back=1)
                        pe.transpose(psX[:, 0:P], xn[:, t.buf(2), :], ident[:, :])
                        pe.transpose(psX[:, P:2 * P], cring[:, t.buf(4), :], ident[:, :]).then_inc(xc_ps, 1)
                    if t := at_step(s, 0):
                        wait_for(pe, v9_done, t, per=4)
                        wait_for(pe, oT_sb, t, back=1)
                        for b in range(2):
                            wait_for(pe, p_sb, t, per=2, part=b)
                            for n in range(PAIRS):
                                g, jp, hp = n // 4, n // 2 % 2, n % 2
                                o = (2 * jp + g) * P + hp * S
                                last = pe.matmul(psO[0:S, b * OROW + n * VW:b * OROW + n * VW + VPAD],
                                                 pT[:, t.buf(2), b, o:o + S],
                                                 v9[:, t.buf(4), b, n * VW:n * VW + VPAD], start=True, stop=True)
                        last.then_inc(pv_ps, 1)
                    if t := at_step(s, 3):
                        wait_for(pe, xc_sb, t)
                        pe.matmul(psX[:, 2 * P:3 * P], wT[:, 0, :], xcT[:, t.buf(2), 0:P], start=True, stop=True).then_inc(q_ps, 1)
                        wait_for(pe, kT_sb, t, back=1)
                        pe.matmul(psK[:, 0:2 * D], xcT[:, t.buf(2), P:2 * P], wT[:, 1:3, :], start=True, stop=True).then_inc(kv_ps, 1)
                    if t := at_step(s, -1):
                        wait_for(pe, zn_done, t)
                        pe.transpose(psG[:, P:2 * P], zn[:, t.buf(2), :], ident[:, :]).then_inc(z_ps, 1)
                    if t := at_step(s, 0):
                        wait_for(pe, on_done, t, per=2)
                        pe.transpose(psO[:, 384:512], on[:, t.buf(2), :], ident[:, :]).then_inc(oT_ps, 1)
                    if t := at_step(s, -1):
                        wait_for(pe, z_sb, t, per=2)
                        pe.matmul(psG[:, 256:384], zTs[:, t.buf(2), :], gatew[:, :], start=True, stop=True).then_inc(lg_ps, 1)

                pipeline(pe, step)

            @block.scalar
            def _(act):
                act.wait_ge(weights_in, 16 * 11)
                nc.scalar.activation(tg[:, :], gcol[:, :], ACT.Tanh).then_inc(tanh_ready, 1)
                act.wait_ge(wT_ps, 1)
                nc.scalar.copy(wT[:, 0:3, :], psS[0][:, 0:3 * D].rearrange("p (a b) -> p a b", a=3)).then_inc(wT_sb, 1)
                act.wait_ge(tanh_ready, 1)
                nc.scalar.activation(wT[:, 3, :], psS[0][:, 3 * D:4 * D], ACT.Copy, scale=tg[:, 0:1]).then_inc(wT_sb, 1)
                act.wait_ge(zero_ready, 4)

                def step(s):
                    if t := at_step(s, -1):
                        wait_for(act, oT_ps, t)
                        wait_for(act, attn_ps, t, back=2)
                        nc.scalar.copy(oT[:, t.buf(2), :], psO[:, 384:512]).then_inc(oT_sb, 1)
                    if t := at_step(s, 0):
                        for b in range(2):
                            wait_for(act, p_ps, t, per=2, part=b)
                            wait_for(act, pv_ps, t, back=2)
                            nc.scalar.copy(pT[:, t.buf(2), b, :], psP[b][:, :]).then_inc(p_sb, 1)
                    if t := at_step(s, 2):
                        wait_for(act, kT_ps, t)
                        wait_for(act, s_ps, t, back=2, per=2)
                        for g in range(4):
                            r = slice(32 * g, 32 * g + 32)
                            last = nc.scalar.copy(kfull[r, t.buf(2), g, :], psK[r, 256:384])
                        last.then_inc(kT_sb, 1)
                    if t := at_step(s, 3):
                        wait_for(act, xc_ps, t)
                        wait_for(act, kv_ps, t, back=2)
                        nc.scalar.copy(xcT[:, t.buf(2), :], psX[:, 0:2 * P]).then_inc(xc_sb, 1)
                    if t := at_step(s, 1):
                        for b in range(2):
                            wait_for(act, sub_done, t, per=2, part=b)
                            wait_for(act, p_ps, t, back=2, per=2)
                            nc.scalar.activation(ex[:, t.buf(2), b, :], sx[:, b, :], ACT.Exp, scale=SCALE).then_inc(exp_done, 1)
                    if t := at_step(s, -1):
                        wait_for(act, z_ps, t)
                        wait_for(act, lg_ps, t, back=2)
                        nc.scalar.copy(zTs[:, t.buf(2), :], psG[:, P:2 * P]).then_inc(z_sb, 1)
                        nc.scalar.copy(one(zT, t), psG[:, P:2 * P]).then_inc(z_sb, 1)

                pipeline(act, step)

            @block.vector
            def _(dve):
                nc.vector.memset(kfull[:, :, :, :], 0.0).then_inc(zero_ready, 1)
                nc.vector.memset(v9[:, :, :, :], 0.0).then_inc(zero_ready, 1)
                nc.vector.memset(gatew[:, :], 0.0).then_inc(zero_ready, 1)
                nc.vector.memset(mhalf[:, :], -0.5).then_inc(zero_ready, 1)
                dve.wait_ge(zero_ready, 4)
                ones = v9[:, :, :, 0:PAIRS * VW].rearrange("p u b (n w) -> p (u b) n w", w=VW)
                nc.vector.memset(ones[0:S, :, :, DH], 1.0)
                nc.vector.memset(ones[S:P, :, :, VW - 1], 1.0).then_inc(ones_ready, 1)
                dve.wait_ge(weights_in, 16 * 11)
                for g in range(2):
                    nc.vector.tensor_copy(wperm[:, g * 64:(g + 1) * 64].rearrange("p (r c w) -> p r c w", r=4, c=2),
                                          wnat[:, 3, g * 64:(g + 1) * 64].rearrange("p (c r w) -> p r c w", r=4, c=2)).then_inc(wp_ready, 1)
                dve.wait_ge(tanh_ready, 1)
                nc.vector.tensor_scalar(bpg[:, :], bp[:, :], tg[:, 0:1], None, ALU.mult).then_inc(bias_ready, 1)

                def step(s):
                    if t := at_step(s, -2):
                        wait_for(dve, lg_ps, t)
                        nc.vector.tensor_copy(one(lg, t), psG[:, 256:256 + E]).then_inc(lg_sb, 1)
                    if t := at_step(s, 2):
                        wait_for(dve, kv_ps, t)
                        wait_for(dve, kr_done, t, back=2)
                        wait_for(dve, v9_done, t, back=2, per=4)
                        kv = psK[:, 0:2 * D].rearrange("p (a f) -> p a f", a=2)
                        cs = cosT[:, :].unsqueeze(1).broadcast_to([P, 2, D])
                        nc.vector.tensor_tensor(ropA[:, t.buf(2), :].rearrange("p (a f) -> p a f", a=2), kv, cs, ALU.mult)
                        swapped = psK[:, 0:2 * D].rearrange("p (a f o) -> p a f o", a=2, o=2)[:, :, :, ::-1]
                        sn = sinT[:, :].rearrange("p (f o) -> p f o", o=2).unsqueeze(1).broadcast_to([P, 2, D // 2, 2])
                        nc.vector.tensor_tensor(ropB[:, t.buf(2), :].rearrange("p (a f o) -> p a f o", a=2, o=2),
                                                swapped, sn, ALU.mult).then_inc(rope_done, 1)
                        wait_for(dve, q_ps, t)
                        wait_for(dve, s_ps, t, back=2, per=2)
                        nc.vector.tensor_tensor(qblk[:, t.buf(2), :, :, :],
                                                psX[:, 2 * P:3 * P].rearrange("p (b q) -> p b q", b=2).unsqueeze(2).broadcast_to([P, 2, 4, S]),
                                                hmask[:, :].unsqueeze(1).unsqueeze(3).broadcast_to([P, 2, 4, S]),
                                                ALU.mult).then_inc(q_sb, 1)
                    if t := at_step(s, 4):
                        wait_for(dve, tiles_in, t, per=32)
                        wait_for(dve, mv1_done, t, back=2)
                        carry(dve)
                        nc.vector.bn_stats(st1[:, t.buf(2), :], one(xres, t)).then_inc(st1_done, 1)
                        wait_for(dve, st1_done, t)
                        wait_for(dve, ve1_done, t, back=2)
                        carry(dve)
                        nc.vector.bn_aggr(mv1[:, t.buf(2), :], st1[:, t.buf(2), :]).then_inc(mv1_done, 1)

                    def softmax_in(b):
                        if t := at_step(s, 1):
                            sc = psS[b][:, :].rearrange("p (n k) -> p n k", k=S)
                            wait_for(dve, s_ps, t, per=2, part=b)
                            nc.vector.tensor_reduce(mx[:, b, :], sc, AX_X, ALU.max).then_inc(mx_done, 1)
                            wait_for(dve, mx_done, t, per=2, part=b)
                            wait_for(dve, exp_done, t, back=1, per=2, part=b)
                            nc.vector.tensor_tensor(sx[:, b, :].rearrange("p (n k) -> p n k", k=S), sc,
                                                    mx[:, b, :].unsqueeze(2).broadcast_to([P, PAIRS, S]),
                                                    ALU.subtract).then_inc(sub_done, 1)

                    softmax_in(0)
                    if t := at_step(s, -1):
                        wait_for(dve, attn_ps, t)
                        wait_for(dve, xb_done, t)
                        nc.vector.tensor_tensor(one(xres, t), psG[:, 0:D], one(xres, t), ALU.add).then_inc(x1_done, 1)
                        wait_for(dve, x1_done, t)
                        carry(dve)
                        nc.vector.bn_stats(st2[:, t.buf(2), :], one(xres, t)).then_inc(st2_done, 1)
                        wait_for(dve, st2_done, t)
                        carry(dve)
                        nc.vector.bn_aggr(mv2[:, t.buf(2), :], st2[:, t.buf(2), :]).then_inc(mv2_done, 1)
                    softmax_in(1)
                    if t := at_step(s, 4):
                        wait_for(dve, rs1_done, t)
                        wait_for(dve, xc_ps, t, back=2)
                        nc.vector.tensor_scalar(xn[:, t.buf(2), :], one(xres, t), mv1[:, t.buf(2), 0:1],
                                                rs1[:, t.buf(2), :], ALU.subtract, ALU.mult).then_inc(xn_done, 1)
                    if t := at_step(s, -1):
                        wait_for(dve, rs2_done, t)
                        wait_for(dve, z_ps, t, back=2)
                        nc.vector.tensor_scalar(zn[:, t.buf(2), :], one(xres, t), mv2[:, t.buf(2), 0:1],
                                                rs2[:, t.buf(2), :], ALU.subtract, ALU.mult).then_inc(zn_done, 1)
                    if t := at_step(s, 0):
                        wait_for(dve, pv_ps, t)
                        wait_for(dve, oT_ps, t, back=2)
                        o = psO[0:S, 0:2 * OROW].rearrange("p (b c) -> p b c", b=2)[:, :, 0:PAIRS * VW] \
                            .rearrange("p b (h w) -> p b h w", w=DH + 1)
                        nc.vector.reciprocal(rden[:, :, :], o[:, :, :, DH]).then_inc(rden_done, 1)
                        wait_for(dve, rden_done, t)
                        for b in range(2):
                            nc.vector.tensor_tensor(on[b * S:(b + 1) * S, t.buf(2), :].rearrange("p (h w) -> p h w", w=DH),
                                                    o[:, b, :, 0:DH],
                                                    rden[:, b, :].unsqueeze(2).broadcast_to([S, H, DH]),
                                                    ALU.mult).then_inc(on_done, 1)

                pipeline(dve, step)

            @block.gpsimd
            def _(pool):
                nc.gpsimd.memset(ident[:, :], 0.0).then_inc(ident_ready, 1)
                pool.wait_ge(ident_ready, 1)
                nc.gpsimd.affine_select(out=ident[:, :], in_=ident[:, :], compare_op=ALU.not_equal, fill=1.0, base=0,
                                        pattern=[[-1, P]], channel_multiplier=1).then_inc(ident_ready, 1)
                pool.wait_ge(zero_ready, 4)
                pool.wait_ge(ones_ready, 1)
                pool.wait_ge(bias_ready, 1)

                def rstd(t, mv, ve, rs, mv_done, ve_done, rs_done, used, per):
                    wait_for(pool, mv_done, t)
                    carry(pool)
                    nc.gpsimd.tensor_scalar(ve[:, t.buf(2), :], mv[:, t.buf(2), 1:2], EPS, None, ALU.add).then_inc(ve_done, 1)
                    wait_for(pool, ve_done, t)
                    wait_for(pool, used, t, back=2, per=per)
                    nc.gpsimd.tensor_tensor(rs[:, t.buf(2), :], ve[:, t.buf(2), :], mhalf[:, :], ALU.pow).then_inc(rs_done, 1)

                def step(s):
                    if t := at_step(s, 2):
                        wait_for(pool, rope_done, t)
                        wait_for(pool, kT_ps, t, back=2)
                        nc.gpsimd.tensor_tensor(kr[:, t.buf(2), :], ropA[:, t.buf(2), 0:D], ropB[:, t.buf(2), 0:D],
                                                ALU.add).then_inc(kr_done, 1)
                    if t := at_step(s, 4):
                        rstd(t, mv1, ve1, rs1, mv1_done, ve1_done, rs1_done, xn_done, 1)
                        wait_for(pool, rs1_done, t)
                    if t := at_step(s, 2):
                        wait_for(pool, pv_ps, t, back=4)
                        for n, (b, c) in enumerate(((0, 0), (0, 1), (1, 0), (1, 1))):
                            src = [r[b * S:(b + 1) * S, t.buf(2), D:2 * D]
                                   .rearrange("p (g c r w) -> p g c r w", g=2, c=2, w=DH)[:, :, c, :, :] for r in (ropA, ropB)]
                            dst = v9[c * S:(c + 1) * S, t.buf(4), b, 0:PAIRS * VW] \
                                .rearrange("p (g r c w) -> p g r c w", g=2, c=2, w=DH + 1)[:, :, :, c, 0:DH]
                            if n >= 1:
                                wait_for(pool, v9_done, t, per=4, part=n - 1)
                            nc.gpsimd.tensor_tensor(dst, src[0], src[1], ALU.add).then_inc(v9_done, 1)
                        wait_for(pool, v9_done, t, per=4)
                    if t := at_step(s, -1):
                        rstd(t, mv2, ve2, rs2, mv2_done, ve2_done, rs2_done, zn_done, 1)
                    if t := at_step(s, 3):
                        wait_for(pool, xn_done, t)
                        nc.gpsimd.tensor_tensor(one(xres, t), one(xres, t), bpg[:, :], ALU.add).then_inc(xb_done, 1)

                pipeline(pool, step)

        feed_forward_dense(nc, ctx, sb, sem, xres, zT, lg, tg, w0, w1, wo, psS + psP, psO, psG, experts_in, o_d)


def feed_forward_dense(nc, ctx, sb, sem, xres, zT, lg, tg, w0, w1, wo, banks, psY0, psY1, experts_in, o_d):
    top, idx = sb("top", [P, NT, 8]), sb("idx", [P, NT, 8], U32)
    idf = sb("idf", [P, NT, 2])
    iot = sb("iot", [P, E])
    pr = sb("pr", [P, NT, 3])
    oh = sb("oh", [P, NT, E])
    wgt = sb("wgt", [P, NT, E])
    hs = sb("hs", [P, 2, 256])
    hT = sb("hT", [P, 2, 2, P])
    gate_step, exp2_done, iota_done = sem("gate_step"), sem("exp2_done"), sem("iota_done")
    h_ps, silu_done, h_sb, y_ps, y_done, out_done = sem("h_ps"), sem("silu_done"), sem("h_sb"), sem("y_ps"), sem("y_done"), sem("out_done")
    psY = [psY0, psY1]

    with nc.Block() as block:
        @block.gpsimd
        def _(pool):
            nc.gpsimd.iota(iot[:, :], pattern=[[1, E]], base=0, channel_multiplier=0,
                           allow_small_or_imprecise_dtypes=True).then_inc(iota_done, 1)

        @block.scalar
        def _(act):
            act.wait_ge(gate_step, 4)
            nc.scalar.activation(pr[:, :, 0], pr[:, :, 2], ACT.Exp).then_inc(exp2_done, 1)
            with act.Fori(0, NT) as t:
                for e in range(E):
                    act.wait_ge(h_ps, E * t + e + 1)
                    if e >= 2:
                        act.wait_ge(h_sb, E * t + e - 1)
                    nc.scalar.activation(hs[:, e % 2, :], banks[e % 4][:, 0:256], ACT.Silu).then_inc(silu_done, 1)

        @block.tensor
        def _(pe):
            pe.wait_ge(experts_in, 16 * (2 + E))
            pe.wait_ge(gate_step, 8)
            with pe.Fori(0, NT) as t:
                z = zT[:, bass.ds(t, 1), :].squeeze(1)

                def up(e):
                    if e >= 4:
                        pe.wait_ge(h_sb, E * t + e - 3)
                    for w, o in ((w0, 0), (w1, 256)):
                        for k in range(2):
                            last = pe.matmul(banks[e % 4][:, o + k * P:o + (k + 1) * P], w[:, e, k * P:(k + 1) * P], z, start=True, stop=True)
                    last.then_inc(h_ps, 1)

                def down(e):
                    pe.wait_ge(h_sb, E * t + e + 1)
                    if e >= 2:
                        pe.wait_ge(y_done, E * t + e - 1)
                    for k in range(2):
                        last = pe.matmul(psY[e % 2][:, 0:D], hT[:, e % 2, k, :], wo[:, e, k, :], start=(k == 0), stop=(k == 1))
                    last.then_inc(y_ps, 1)

                up(0)
                for e in range(1, E):
                    up(e)
                    down(e - 1)
                down(E - 1)
                pe.wait_ge(y_done, E * t + E)

        @block.vector
        def _(dve):
            for t in range(NT):
                nc.vector.max(top[:, t, :], lg[:, t, :])
            last = nc.vector.memset(wgt[:, :, :], 0.0)
            last.then_inc(gate_step, 1)
            dve.wait_ge(gate_step, 1)
            for t in range(NT):
                last = nc.vector.max_index(idx[:, t, :], top[:, t, :], lg[:, t, :])
            last.then_inc(gate_step, 1)
            dve.wait_ge(gate_step, 2)
            nc.vector.tensor_copy(idf[:, :, :], idx[:, :, 0:2]).then_inc(gate_step, 1)
            nc.vector.tensor_tensor(pr[:, :, 2], top[:, :, 1], top[:, :, 0], ALU.subtract).then_inc(gate_step, 1)
            dve.wait_ge(exp2_done, 1)
            nc.vector.tensor_scalar(pr[:, :, 2], pr[:, :, 0], 1.0, None, ALU.add).then_inc(gate_step, 1)
            dve.wait_ge(gate_step, 5)
            nc.vector.reciprocal(pr[:, :, 1], pr[:, :, 2]).then_inc(gate_step, 1)
            dve.wait_ge(gate_step, 6)
            nc.vector.tensor_scalar(pr[:, :, 1], pr[:, :, 1], tg[:, 1:2], None, ALU.mult).then_inc(gate_step, 1)
            dve.wait_ge(gate_step, 7)
            nc.vector.tensor_tensor(pr[:, :, 0], pr[:, :, 1], pr[:, :, 0], ALU.mult).then_inc(gate_step, 1)
            dve.wait_ge(gate_step, 8)
            dve.wait_ge(iota_done, 1)
            n = 8
            for j, c in ((0, 1), (1, 0)):
                nc.vector.tensor_tensor(oh[:, :, :], iot[:, :].unsqueeze(1).broadcast_to([P, NT, E]),
                                        idf[:, :, j:j + 1].broadcast_to([P, NT, E]), ALU.is_equal).then_inc(gate_step, 1)
                n += 1
                dve.wait_ge(gate_step, n)
                nc.vector.tensor_tensor(oh[:, :, :], oh[:, :, :], pr[:, :, c:c + 1].broadcast_to([P, NT, E]), ALU.mult).then_inc(gate_step, 1)
                n += 1
                dve.wait_ge(gate_step, n)
                nc.vector.tensor_tensor(wgt[:, :, :], wgt[:, :, :], oh[:, :, :], ALU.add).then_inc(gate_step, 1)
                n += 1
                dve.wait_ge(gate_step, n)
            with dve.Fori(0, NT) as t:
                x1 = xres[:, bass.ds(t, 1), :].squeeze(1)
                wt = wgt[:, bass.ds(t, 1), :].squeeze(1)

                def mult(e):
                    dve.wait_ge(silu_done, E * t + e + 1)
                    if e >= 2:
                        dve.wait_ge(y_ps, E * t + e - 1)
                    nc.vector.tensor_tensor(hT[:, e % 2, :, :], banks[e % 4][:, 256:512].rearrange("p (k c) -> p k c", k=2),
                                            hs[:, e % 2, :].rearrange("p (k c) -> p k c", k=2), ALU.mult).then_inc(h_sb, 1)

                def add(e):
                    dve.wait_ge(y_ps, E * t + e + 1)
                    if e:
                        dve.wait_ge(y_done, E * t + e)
                    nc.vector.scalar_tensor_tensor(out=x1, in0=psY[e % 2][:, 0:D], scalar=wt[:, e:e + 1], in1=x1,
                                                   op0=ALU.mult, op1=ALU.add).then_inc(y_done, 1)

                mult(0)
                for e in range(1, E):
                    mult(e)
                    add(e - 1)
                add(E - 1)

        @block.sync
        def _(sp):
            with sp.Fori(0, NT) as t:
                sp.wait_ge(y_done, E * t + E)
                carry(sp)
                sp.dma_start(o_d[:, bass.ds(t, 1), :].squeeze(1), xres[:, bass.ds(t, 1), :].squeeze(1)).then_inc(out_done, 16)
            sp.wait_ge(out_done, 16 * NT)


_INS = ["x", "ctx_1024", "g_xattn", "g_ffn", "L0_xattn_Wq", "L0_xattn_Wk", "L0_xattn_Wv", "L0_xattn_Wp", "L0_xattn_bp",
        "L0_ffn_gate_kernel", "L0_ffn_w0_kernel", "L0_ffn_w1_kernel", "L0_ffn_wo_kernel"]


def shape_constants():
    import numpy as np
    theta = (np.float32(1.0) / np.float32(10000.0) ** (np.float32(2.0) * np.arange(D // 2, dtype=np.float32) / np.float32(D))).astype(np.float32)
    ang = np.arange(S, dtype=np.float32)[:, None] * theta[None, :]
    cos, sin = np.cos(ang), np.sin(ang)
    cos2 = np.repeat(cos, 2, axis=1)
    sin2 = np.stack([-sin, sin], axis=-1).reshape(S, D)
    mask = (np.arange(D)[:, None] // DH % 4 == np.arange(4)[None, :])
    return {"rope_cos": np.tile(cos2, (P // S, 1)).astype(np.float32), "rope_sin": np.tile(sin2, (P // S, 1)).astype(np.float32),
            "head_mask": mask.astype(np.float32)}


def kernel(**inputs):
    import numpy as _np
    import concourse.bacc as _bacc
    from concourse import mybir as _mybir
    from concourse.bass_utils import run_bass_kernel_spmd as _run

    nc = _bacc.Bacc("TRN2", target_bir_lowering=False, num_devices=1)
    arrays, args = {}, {}
    for name, a in [(n, inputs[n]) for n in _INS] + list(shape_constants().items()):
        a = _np.ascontiguousarray(a)
        arrays[f"in_{name}_dram"] = a
        args[name] = nc.dram_tensor(f"in_{name}_dram", a.shape, _mybir.dt.from_np(a.dtype), kind="ExternalInput").ap()
    out = nc.dram_tensor("out_0_dram", (NB, S, D), F32, kind="ExternalOutput").ap()
    flamingo_block(nc, args, out)
    r = _run(nc, [arrays], core_ids=[0])
    return r.results[0]["out_0_dram"]
```

```python
from contextlib import ExitStack

import concourse.bass as bass
from concourse import mybir

F32 = mybir.dt.float32
BF16 = mybir.dt.bfloat16
U32 = mybir.dt.uint32
ALU = mybir.AluOpType
ACT = mybir.ActivationFunctionType
AX_X = mybir.AxisListType.X

P = 128
NB, S, D = 128, 64, 128
H, DH = 16, 8
NT = NB * S // P
PAIRS = H // 2
E, HID = 8, 256
CAP = NT * P + P
SPARE = E
ZROWS = E * CAP + SPARE * P
ROW = D + 2
NET = 2 * NT + E
NOWHERE = 2 * NT * P
EPS = 1e-5
SCALE = float(DH) ** -0.5
VW = 2 * (DH + 1)
VPAD = 64
VROW = (PAIRS - 1) * VW + VPAD
OROW = 192


class Tile:

    def __init__(self, unroll, turn, k):
        self.unroll, self.turn, self.k = unroll, turn, k
        self.val = k if turn is None else unroll * turn + k

    @property
    def lap(self):
        return self.k // self.unroll + (0 if self.turn is None else self.turn)

    def buf(self, n):
        return self.k % n

    def __add__(self, n):
        return Tile(self.unroll, self.turn, self.k + n)


class Pipeline:

    def __init__(self, tiles, behind, ahead, unroll, steady):
        self.tiles, self.unroll, self.steady = tiles, unroll, steady
        self.first, self.last = -ahead, tiles - 1 + behind
        self.turns = (tiles - ahead - steady) // unroll

    def at(self, step, off):
        turn, u = step
        if turn is None:
            return Tile(self.unroll, None, u + off) if 0 <= u + off < self.tiles else None
        return Tile(self.unroll, turn, self.steady + u + off)

    def run(self, eng, body):
        for t in range(self.first, self.steady):
            body((None, t))
        with eng.Fori(0, self.turns) as turn:
            for u in range(self.unroll):
                body((turn, u))
        for t in range(self.steady + self.unroll * self.turns, self.last + 1):
            body((None, t))


ATTENTION = Pipeline(NT, behind=4, ahead=4, unroll=4, steady=9)
EXPERTS = Pipeline(NET, behind=2, ahead=2, unroll=8, steady=10)
CHUNK = 4
COMBINE = Pipeline(NT // CHUNK, behind=0, ahead=0, unroll=4, steady=4)


def wait_for(eng, sem, t, back=0, per=1, part=None):
    v = per * (t.val - back) + (per if part is None else part + 1)
    if isinstance(v, int) and v <= 0:
        return
    eng.wait_ge(sem, v)


def wait_slot(eng, sems, t, per, back=0):
    v = per * (t.lap + 1 - back // t.unroll)
    if isinstance(v, int) and v <= 0:
        return
    eng.wait_ge(sems[t.buf(t.unroll)], v)


def carry(eng):
    eng.nop(nofuse=True)


def flamingo_block(nc, A, out):
    with ExitStack() as ctx:
        def sb(name, shape, dt=F32):
            return ctx.enter_context(nc.sbuf_tensor(name, shape, dt))

        def ps(name):
            return ctx.enter_context(nc.psum_tensor(name, [P, 512], F32))

        def sem(name):
            return ctx.enter_context(nc.semaphore(name))

        xres = sb("xres", [P, NT, D])
        cring = sb("cring", [P, 4, D])
        ident = sb("ident", [P, P])
        wnat = sb("wnat", [P, 4, D])
        wT = sb("wT", [P, 4, D])
        wperm = sb("wperm", [P, D])
        cosT = sb("cosT", [P, D])
        sinT = sb("sinT", [P, D])
        hmask = sb("hmask", [P, 4])
        gcol = sb("gcol", [P, 2])
        tg = sb("tg", [P, 2])
        bp = sb("bp", [P, D])
        bpg = sb("bpg", [P, D])
        mhalf = sb("mhalf", [P, 2])
        gatew = sb("gatew", [P, D])
        w01 = sb("w01", [P, E, 2, HID])
        wo = sb("wo", [P, E, 2, D])
        st1, st2 = sb("st1", [P, 2, 6]), sb("st2", [P, 2, 6])
        mv1, mv2 = sb("mv1", [P, 4, 2]), sb("mv2", [P, 2, 2])
        ve1, ve2 = sb("ve1", [P, 4]), sb("ve2", [P, 2, 1])
        rs1, rs2 = sb("rs1", [P, 4]), sb("rs2", [P, 2, 1])
        xn = sb("xn", [P, 2, D])
        xcT = sb("xcT", [P, 2, 2 * D])
        ropA = sb("ropA", [P, 2, 2 * D])
        ropB = sb("ropB", [P, 2, 2 * D])
        kvr = sb("kvr", [P, 2, 2 * D])
        qblk = sb("qblk", [P, 2, 2, 4, S])
        kfull = sb("kfull", [P, 2, 4, D])
        v9 = sb("v9", [P, 4, 2, VROW])
        sx = sb("sx", [P, 2, 512])
        ex = sb("ex", [P, 2, 2, 512])
        mx = sb("mx", [P, 2, PAIRS])
        pT = sb("pT", [P, 2, 2, 512])
        rden = sb("rden", [S, 2, 2 * PAIRS])
        on = sb("on", [P, 2, D])
        oT = sb("oT", [P, 2, D])
        zp = sb("zp", [P, 4, 2, ROW])
        zTs = sb("zTs", [P, 2, D])
        top = sb("top", [P, 4, 8])
        idx = sb("idx", [P, 4, 8], U32)
        idf = sb("idf", [P, 2, 2, 2])
        gap = sb("gap", [P, 2, 2])
        egap = sb("egap", [P, 2, 2])
        den2 = sb("den2", [P, 2])
        rden2 = sb("rden2", [P, 2])
        iot = sb("iot", [P, E])
        base = sb("base", [P, E])
        oh = sb("oh", [P, 2, 2, 2, E])
        chosen = sb("chosen", [P, 2, 2, E], BF16)
        before = sb("before", [P, 2, 2, E], BF16)
        place = sb("place", [P, 2, E])
        hit = sb("hit", [P, 2, 2, E])
        dest = sb("dest", [P, 2, 2, 2], U32)
        tokid = sb("tokid", [P, NT, 2], U32)
        lower = sb("lower", [P, P], BF16)
        allone = sb("allone", [P, P], BF16)

        psS = [ps("psS0"), ps("psS1")]
        psP = [ps("psP0"), ps("psP1")]
        psX = ps("psX")
        psK = ps("psK")
        psO = ps("psO")
        psG = ps("psG")

        weights_in, experts_in, tiles_in = sem("weights_in"), sem("experts_in"), sem("tiles_in")
        ident_ready, zero_ready, ones_ready = sem("ident_ready"), sem("zero_ready"), sem("ones_ready")
        wp_ready = sem("wp_ready")
        wT_ps, wT_sb, tanh_ready, bias_ready, half_ready = sem("wT_ps"), sem("wT_sb"), sem("tanh_ready"), sem("bias_ready"), sem("half_ready")
        st1_done, mv1_done, ve1_done, rs1_done = sem("st1_done"), sem("mv1_done"), sem("ve1_done"), sem("rs1_done")
        xn_done, xb_done, xc_ps, xc_sb = sem("xn_done"), sem("xb_done"), sem("xc_ps"), sem("xc_sb")
        q_ps, kv_ps, q_sb, rope_done = sem("q_ps"), sem("kv_ps"), sem("q_sb"), sem("rope_done")
        v9_done, kT_ps, kT_sb = sem("v9_done"), sem("kT_ps"), sem("kT_sb")
        s_ps, mx_done, sub_done, exp_done = sem("s_ps"), sem("mx_done"), sem("sub_done"), sem("exp_done")
        p_ps, p_sb, pv_ps, rden_done, on_done = sem("p_ps"), sem("p_sb"), sem("pv_ps"), sem("rden_done"), sem("on_done")
        oT_ps, oT_sb, attn_ps, x1_done = sem("oT_ps"), sem("oT_sb"), sem("attn_ps"), sem("x1_done")
        st2_done, mv2_done, ve2_done, rs2_done = sem("st2_done"), sem("mv2_done"), sem("ve2_done"), sem("rs2_done")
        zn_done, z_ps, z_sb, lg_ps, lg_sb = sem("zn_done"), sem("z_ps"), sem("z_sb"), sem("lg_ps"), sem("lg_sb")
        kvr_done, z2_done, top_done, idf_done = sem("kvr_done"), sem("z2_done"), sem("top_done"), sem("idf_done")
        oh_done, gap_done, egap_done, chosen_done = sem("oh_done"), sem("gap_done"), sem("egap_done"), sem("chosen_done")
        before_done, place_ps, den2_done, rden2_done = sem("before_done"), sem("place_ps"), sem("den2_done"), sem("rden2_done")
        weight_done, place_done, hit_done, dest_done = sem("weight_done"), sem("place_done"), sem("hit_done"), sem("dest_done")
        tok_done, route_ready, pad_ready, spare_out = sem("tok_done"), sem("route_ready"), sem("pad_ready"), sem("spare_out")
        row_out = [sem(f"row_out{i}") for i in range(4)]

        x_d = A["x"].rearrange("b s d -> (b s) d").rearrange("(t p) d -> p t d", p=P)
        c_d = A["ctx_1024"].rearrange("b s d -> (b s) d").rearrange("(t p) d -> p t d", p=P)
        o_d = out.rearrange("b s d -> (b s) d").rearrange("(t p) d -> p t d", p=P)

        def one(ap, t):
            return ap[:, t.val, :] if isinstance(t.val, int) else ap[:, bass.ds(t.val, 1), :].squeeze(1)

        with nc.Block() as block:
            @block.sync
            def _(sp):
                for n, w in enumerate(("L0_xattn_Wq", "L0_xattn_Wk", "L0_xattn_Wv", "L0_xattn_Wp")):
                    sp.dma_start(wnat[:, n, :], A[w]).then_inc(weights_in, 16)
                sp.dma_start(cosT[:, :], A["rope_cos"]).then_inc(weights_in, 16)
                sp.dma_start(sinT[:, :], A["rope_sin"]).then_inc(weights_in, 16)
                sp.dma_start(hmask[:, :], A["head_mask"]).then_inc(weights_in, 16)
                sp.dma_start(gcol[:, 0:1], A["g_xattn"].unsqueeze(0).broadcast_to([P, 1])).then_inc(weights_in, 16)
                sp.dma_start(gcol[:, 1:2], A["g_ffn"].unsqueeze(0).broadcast_to([P, 1])).then_inc(weights_in, 16)
                sp.dma_start(bp[:, :], A["L0_xattn_bp"].unsqueeze(0).broadcast_to([P, D])).then_inc(weights_in, 16)
                sp.wait_ge(zero_ready, 4)
                sp.dma_start(gatew[:, 0:E], A["L0_ffn_gate_kernel"]).then_inc(weights_in, 16)

                def load(t):
                    wait_for(sp, tiles_in, t, back=1, per=32)
                    carry(sp)
                    wait_for(sp, xc_ps, t, back=4)
                    carry(sp)
                    sp.dma_start(one(xres, t), one(x_d, t)).then_inc(tiles_in, 16)
                    sp.dma_start(cring[:, t.buf(4), :], one(c_d, t)).then_inc(tiles_in, 16)

                for t in range(4):
                    load(Tile(4, None, t))
                with sp.Fori(1, NT // 4) as turn:
                    for u in range(4):
                        load(Tile(4, turn, u))
                sp.dma_start(w01[:, :, 0, :], A["L0_ffn_w0_kernel"].rearrange("e d h -> d e h")).then_inc(experts_in, 16)
                sp.dma_start(w01[:, :, 1, :], A["L0_ffn_w1_kernel"].rearrange("e d h -> d e h")).then_inc(experts_in, 16)
                for e in range(E):
                    sp.dma_start(wo[:, e, :, :], A["L0_ffn_wo_kernel"][e].rearrange("(k h) d -> h k d", k=2)).then_inc(experts_in, 16)

            @block.tensor
            def _(pe):
                pe.wait_ge(weights_in, 16 * 11)
                pe.wait_ge(ident_ready, 2)
                pe.wait_ge(wp_ready, 2)
                for n in range(4):
                    last = pe.transpose(psS[0][:, n * D:(n + 1) * D], wnat[:, n, :] if n < 3 else wperm[:, :], ident[:, :])
                last.then_inc(wT_ps, 1)
                pe.wait_ge(wT_sb, 2)
                pe.wait_ge(ones_ready, 1)
                pe.wait_ge(route_ready, 5)

                def step(s):
                    if t := ATTENTION.at(s, 1):
                        wait_for(pe, kT_sb, t)
                        wait_for(pe, q_sb, t)
                        for b in range(2):
                            wait_for(pe, sub_done, t, back=1, per=2, part=b)
                            for jp in range(2):
                                last = pe.matmul(psS[b][:, jp * 256:(jp + 1) * 256],
                                                 qblk[:, t.buf(2), b, 2 * jp:2 * jp + 2, :].rearrange("p j q -> p (j q)"),
                                                 kfull[:, t.buf(2), :, b * S:(b + 1) * S], start=True, stop=True)
                            last.then_inc(s_ps, 1)
                    if t := ATTENTION.at(s, -1):
                        wait_for(pe, oT_sb, t)
                        wait_for(pe, lg_sb, t, back=1)
                        pe.matmul(psG[:, 0:D], oT[:, t.buf(2), :], wT[:, 3, :], start=True, stop=True).then_inc(attn_ps, 1)
                    if t := ATTENTION.at(s, 0):
                        for b in range(2):
                            wait_for(pe, exp_done, t, per=2, part=b)
                            wait_for(pe, p_sb, t, back=1, per=2, part=b)
                            for n in range(4):
                                last = pe.transpose(psP[b][:, n * P:(n + 1) * P],
                                                    ex[:, t.buf(2), b, n * P:(n + 1) * P], ident[:, :])
                            last.then_inc(p_ps, 1)
                    if t := ATTENTION.at(s, 2):
                        wait_for(pe, kvr_done, t)
                        pe.transpose(psK[:, 256:384], kvr[:, t.buf(2), 0:D], ident[:, :]).then_inc(kT_ps, 1)
                    if t := ATTENTION.at(s, 3):
                        wait_for(pe, xn_done, t)
                        wait_for(pe, tiles_in, t, per=32)
                        wait_for(pe, q_sb, t, back=1)
                        pe.transpose(psX[:, 0:P], xn[:, t.buf(2), :], ident[:, :])
                        pe.transpose(psX[:, P:2 * P], cring[:, t.buf(4), :], ident[:, :]).then_inc(xc_ps, 1)
                    if t := ATTENTION.at(s, 0):
                        wait_for(pe, v9_done, t, per=4)
                        wait_for(pe, oT_sb, t, back=1)
                        for b in range(2):
                            wait_for(pe, p_sb, t, per=2, part=b)
                            for n in range(PAIRS):
                                g, jp, hp = n // 4, n // 2 % 2, n % 2
                                o = (2 * jp + g) * P + hp * S
                                last = pe.matmul(psO[0:S, b * OROW + n * VW:b * OROW + n * VW + VPAD],
                                                 pT[:, t.buf(2), b, o:o + S],
                                                 v9[:, t.buf(4), b, n * VW:n * VW + VPAD], start=True, stop=True)
                        last.then_inc(pv_ps, 1)
                    if t := ATTENTION.at(s, 3):
                        wait_for(pe, xc_sb, t)
                        pe.matmul(psX[:, 2 * P:3 * P], wT[:, 0, :], xcT[:, t.buf(2), 0:P], start=True, stop=True).then_inc(q_ps, 1)
                        wait_for(pe, kT_sb, t, back=1)
                        pe.matmul(psK[:, 0:2 * D], xcT[:, t.buf(2), P:2 * P], wT[:, 1:3, :], start=True, stop=True).then_inc(kv_ps, 1)
                    if t := ATTENTION.at(s, -1):
                        wait_for(pe, zn_done, t)
                        pe.transpose(psG[:, P:2 * P], zp[:, t.buf(4), 0, 0:D], ident[:, :]).then_inc(z_ps, 1)
                    if (t := ATTENTION.at(s, -2)) and t.buf(2):
                        q = t.buf(4) // 2
                        wait_for(pe, chosen_done, t)
                        wait_for(pe, before_done, t)
                        if n := ATTENTION.at(s, -1):
                            wait_for(pe, z_sb, n)
                        pe.matmul(psG[:, 384:384 + 2 * E], lower[:, :], chosen[:, q, :, :], start=True, stop=False)
                        pe.matmul(psG[:, 384:384 + 2 * E], allone[:, :], before[:, q, :, :], start=False, stop=True).then_inc(place_ps, 2)
                    if t := ATTENTION.at(s, 0):
                        wait_for(pe, on_done, t, per=2)
                        pe.transpose(psO[:, 384:512], on[:, t.buf(2), :], ident[:, :]).then_inc(oT_ps, 1)
                    if t := ATTENTION.at(s, -1):
                        wait_for(pe, z_sb, t)
                        pe.matmul(psG[:, 256:384], zTs[:, t.buf(2), :], gatew[:, :], start=True, stop=True).then_inc(lg_ps, 1)

                ATTENTION.run(pe, step)

            @block.scalar
            def _(act):
                act.wait_ge(weights_in, 16 * 11)
                nc.scalar.activation(tg[:, :], gcol[:, :], ACT.Tanh).then_inc(tanh_ready, 1)
                act.wait_ge(wT_ps, 1)
                nc.scalar.copy(wT[:, 0:3, :], psS[0][:, 0:3 * D].rearrange("p (a b) -> p a b", a=3)).then_inc(wT_sb, 1)
                act.wait_ge(tanh_ready, 1)
                nc.scalar.activation(wT[:, 3, :], psS[0][:, 3 * D:4 * D], ACT.Copy, scale=tg[:, 0:1]).then_inc(wT_sb, 1)
                act.wait_ge(zero_ready, 4)

                def step(s):
                    if t := ATTENTION.at(s, -1):
                        wait_for(act, oT_ps, t)
                        wait_for(act, attn_ps, t, back=2)
                        nc.scalar.copy(oT[:, t.buf(2), :], psO[:, 384:512]).then_inc(oT_sb, 1)
                    if t := ATTENTION.at(s, 0):
                        for b in range(2):
                            wait_for(act, p_ps, t, per=2, part=b)
                            wait_for(act, pv_ps, t, back=2)
                            nc.scalar.copy(pT[:, t.buf(2), b, :], psP[b][:, :]).then_inc(p_sb, 1)
                    if t := ATTENTION.at(s, 2):
                        wait_for(act, kT_ps, t)
                        wait_for(act, s_ps, t, back=2, per=2)
                        for g in range(4):
                            r = slice(32 * g, 32 * g + 32)
                            last = nc.scalar.copy(kfull[r, t.buf(2), g, :], psK[r, 256:384])
                        last.then_inc(kT_sb, 1)
                    if t := ATTENTION.at(s, 3):
                        wait_for(act, xc_ps, t)
                        wait_for(act, kv_ps, t, back=2)
                        nc.scalar.copy(xcT[:, t.buf(2), :], psX[:, 0:2 * P]).then_inc(xc_sb, 1)
                    if t := ATTENTION.at(s, 2):
                        wait_for(act, kvr_done, t)
                        wait_for(act, pv_ps, t, back=4)
                        for b in range(2):
                            for c in range(2):
                                src = kvr[b * S:(b + 1) * S, t.buf(2), D:2 * D] \
                                    .rearrange("p (g c r w) -> p g c r w", g=2, c=2, w=DH)[:, :, c, :, :]
                                dst = v9[c * S:(c + 1) * S, t.buf(4), b, 0:PAIRS * VW] \
                                    .rearrange("p (g r c w) -> p g r c w", g=2, c=2, w=DH + 1)[:, :, :, c, 0:DH]
                                nc.scalar.copy(dst, src).then_inc(v9_done, 1)
                    if t := ATTENTION.at(s, 1):
                        for b in range(2):
                            wait_for(act, sub_done, t, per=2, part=b)
                            wait_for(act, p_ps, t, back=2, per=2)
                            nc.scalar.activation(ex[:, t.buf(2), b, :], sx[:, b, :], ACT.Exp, scale=SCALE).then_inc(exp_done, 1)
                    if t := ATTENTION.at(s, -1):
                        wait_for(act, z_ps, t)
                        wait_for(act, lg_ps, t, back=2)
                        nc.scalar.copy(zTs[:, t.buf(2), :], psG[:, P:2 * P]).then_inc(z_sb, 1)
                        nc.scalar.copy(zp[:, t.buf(4), 1, 0:D], zp[:, t.buf(4), 0, 0:D]).then_inc(z2_done, 1)
                    if (t := ATTENTION.at(s, -2)) and t.buf(2):
                        wait_for(act, gap_done, t)
                        wait_for(act, weight_done, t, back=4)
                        nc.scalar.activation(egap[:, t.buf(4) // 2, :], gap[:, t.buf(4) // 2, :], ACT.Exp).then_inc(egap_done, 2)

                ATTENTION.run(act, step)

            @block.vector
            def _(dve):
                nc.vector.memset(kfull[:, :, :, :], 0.0).then_inc(zero_ready, 1)
                nc.vector.memset(v9[:, :, :, :], 0.0).then_inc(zero_ready, 1)
                nc.vector.memset(gatew[:, :], 0.0).then_inc(zero_ready, 1)
                nc.vector.memset(mhalf[:, :], -0.5).then_inc(zero_ready, 1)
                dve.wait_ge(zero_ready, 4)
                ones = v9[:, :, :, 0:PAIRS * VW].rearrange("p u b (n w) -> p (u b) n w", w=VW)
                nc.vector.memset(ones[0:S, :, :, DH], 1.0)
                nc.vector.memset(ones[S:P, :, :, VW - 1], 1.0).then_inc(ones_ready, 1)
                dve.wait_ge(weights_in, 16 * 11)
                for g in range(2):
                    nc.vector.tensor_copy(wperm[:, g * 64:(g + 1) * 64].rearrange("p (r c w) -> p r c w", r=4, c=2),
                                          wnat[:, 3, g * 64:(g + 1) * 64].rearrange("p (c r w) -> p r c w", r=4, c=2)).then_inc(wp_ready, 1)
                dve.wait_ge(tanh_ready, 1)
                nc.vector.tensor_scalar(bpg[:, :], bp[:, :], tg[:, 0:1], None, ALU.mult).then_inc(bias_ready, 1)
                dve.wait_ge(route_ready, 5)

                def step(s):
                    if (t := ATTENTION.at(s, -3)) and t.buf(2):
                        q, r = t.buf(4) // 2, slice(t.buf(4) - 1, t.buf(4) + 1)
                        wait_for(dve, place_ps, t)
                        if n := ATTENTION.at(s, -2):
                            wait_for(dve, lg_ps, n)
                        nc.vector.tensor_tensor(place[:, :, :], psG[:, 384:384 + 2 * E].rearrange("p (u e) -> p u e", u=2),
                                                base[:, :].unsqueeze(1).broadcast_to([P, 2, E]), ALU.add).then_inc(place_done, 2)
                        wait_for(dve, egap_done, t)
                        nc.vector.tensor_scalar(den2[:, :], egap[:, q, :], 1.0, None, ALU.add).then_inc(den2_done, 2)
                        wait_for(dve, place_done, t)
                        nc.vector.tensor_tensor(hit[:, :, :, :], oh[:, q, :, :, :],
                                                place[:, :, :].unsqueeze(2).broadcast_to([P, 2, 2, E]), ALU.mult).then_inc(hit_done, 2)
                        wait_for(dve, den2_done, t)
                        nc.vector.reciprocal(rden2[:, :], den2[:, :]).then_inc(rden2_done, 2)
                        wait_for(dve, hit_done, t)
                        for i in (1, 0):
                            wait_slot(dve, row_out, t + -i, 32, back=4)
                        with nc.allow_low_precision(reason="a row's number: whole and below 2**24"):
                            nc.vector.tensor_reduce(dest[:, q, :, :], hit[:, :, :, :], AX_X, ALU.add).then_inc(dest_done, 2)
                        wait_for(dve, rden2_done, t)
                        nc.vector.tensor_scalar(zp[:, r, 0, D + 1], rden2[:, :], tg[:, 1:2], None, ALU.mult).then_inc(weight_done, 1)
                        nc.vector.scalar_tensor_tensor(out=zp[:, r, 1, D + 1], in0=rden2[:, :], scalar=tg[:, 1:2],
                                                       in1=egap[:, q, :], op0=ALU.mult, op1=ALU.mult).then_inc(weight_done, 1)
                    if t := ATTENTION.at(s, -2):
                        wait_for(dve, lg_ps, t)
                        carry(dve)
                        nc.vector.max(top[:, t.buf(4), :], psG[:, 256:256 + E]).then_inc(top_done, 1)
                        wait_for(dve, top_done, t)
                        carry(dve)
                        nc.vector.max_index(idx[:, t.buf(4), :], top[:, t.buf(4), :], psG[:, 256:256 + E]).then_inc(lg_sb, 1)
                    if (t := ATTENTION.at(s, -2)) and t.buf(2):
                        q, r = t.buf(4) // 2, slice(t.buf(4) - 1, t.buf(4) + 1)
                        wait_for(dve, egap_done, t, back=4)
                        nc.vector.tensor_tensor(gap[:, q, :], top[:, r, 1], top[:, r, 0], ALU.subtract).then_inc(gap_done, 2)
                        wait_for(dve, lg_sb, t)
                        nc.vector.tensor_copy(idf[:, q, :, :], idx[:, r, 0:2]).then_inc(idf_done, 2)
                        wait_for(dve, idf_done, t)
                        nc.vector.tensor_tensor(oh[:, q, :, :, :], iot[:, :].unsqueeze(1).unsqueeze(1).broadcast_to([P, 2, 2, E]),
                                                idf[:, q, :, :].unsqueeze(3).broadcast_to([P, 2, 2, E]), ALU.is_equal).then_inc(oh_done, 2)
                        wait_for(dve, oh_done, t)
                        wait_for(dve, place_ps, t, back=4)
                        nc.vector.tensor_tensor(chosen[:, q, :, :], oh[:, q, :, 0, :], oh[:, q, :, 1, :], ALU.add).then_inc(chosen_done, 2)
                    if t := ATTENTION.at(s, 2):
                        wait_for(dve, kv_ps, t)
                        wait_for(dve, kvr_done, t, back=2)
                        kv = psK[:, 0:2 * D].rearrange("p (a f) -> p a f", a=2)
                        cs = cosT[:, :].unsqueeze(1).broadcast_to([P, 2, D])
                        nc.vector.tensor_tensor(ropA[:, t.buf(2), :].rearrange("p (a f) -> p a f", a=2), kv, cs, ALU.mult)
                        swapped = psK[:, 0:2 * D].rearrange("p (a f o) -> p a f o", a=2, o=2)[:, :, :, ::-1]
                        sn = sinT[:, :].rearrange("p (f o) -> p f o", o=2).unsqueeze(1).broadcast_to([P, 2, D // 2, 2])
                        nc.vector.tensor_tensor(ropB[:, t.buf(2), :].rearrange("p (a f o) -> p a f o", a=2, o=2),
                                                swapped, sn, ALU.mult).then_inc(rope_done, 1)
                        wait_for(dve, q_ps, t)
                        wait_for(dve, s_ps, t, back=2, per=2)
                        nc.vector.tensor_tensor(qblk[:, t.buf(2), :, :, :],
                                                psX[:, 2 * P:3 * P].rearrange("p (b q) -> p b q", b=2).unsqueeze(2).broadcast_to([P, 2, 4, S]),
                                                hmask[:, :].unsqueeze(1).unsqueeze(3).broadcast_to([P, 2, 4, S]),
                                                ALU.mult).then_inc(q_sb, 1)
                    if (u := ATTENTION.at(s, 4)) and not u.buf(2):
                        wait_for(dve, tiles_in, u + 1, per=32)
                        wait_for(dve, mv1_done, u, back=1)
                        for t in (u, u + 1):
                            carry(dve)
                            nc.vector.bn_stats(st1[:, t.buf(2), :], one(xres, t)).then_inc(st1_done, 1)
                        for t in (u, u + 1):
                            wait_for(dve, st1_done, t)
                            carry(dve)
                            nc.vector.bn_aggr(mv1[:, t.buf(4), :], st1[:, t.buf(2), :]).then_inc(mv1_done, 1)

                    def softmax_in(b):
                        if t := ATTENTION.at(s, 1):
                            sc = psS[b][:, :].rearrange("p (n k) -> p n k", k=S)
                            wait_for(dve, s_ps, t, per=2, part=b)
                            nc.vector.tensor_reduce(mx[:, b, :], sc, AX_X, ALU.max).then_inc(mx_done, 1)
                            wait_for(dve, mx_done, t, per=2, part=b)
                            wait_for(dve, exp_done, t, back=1, per=2, part=b)
                            nc.vector.tensor_tensor(sx[:, b, :].rearrange("p (n k) -> p n k", k=S), sc,
                                                    mx[:, b, :].unsqueeze(2).broadcast_to([P, PAIRS, S]),
                                                    ALU.subtract).then_inc(sub_done, 1)

                    softmax_in(0)
                    if t := ATTENTION.at(s, -1):
                        wait_for(dve, attn_ps, t)
                        wait_for(dve, xb_done, t)
                        nc.vector.tensor_tensor(one(xres, t), psG[:, 0:D], one(xres, t), ALU.add).then_inc(x1_done, 1)
                        wait_for(dve, x1_done, t)
                        carry(dve)
                        nc.vector.bn_stats(st2[:, t.buf(2), :], one(xres, t)).then_inc(st2_done, 1)
                        wait_for(dve, st2_done, t)
                        carry(dve)
                        nc.vector.bn_aggr(mv2[:, t.buf(2), :], st2[:, t.buf(2), :]).then_inc(mv2_done, 1)
                    softmax_in(1)
                    if t := ATTENTION.at(s, 4):
                        wait_for(dve, rs1_done, t)
                        wait_for(dve, xc_ps, t, back=2)
                        nc.vector.tensor_scalar(xn[:, t.buf(2), :], one(xres, t), mv1[:, t.buf(4), 0:1],
                                                rs1[:, t.buf(4):t.buf(4) + 1], ALU.subtract, ALU.mult).then_inc(xn_done, 1)
                    if t := ATTENTION.at(s, -1):
                        wait_for(dve, rs2_done, t)
                        wait_slot(dve, row_out, t, 32, back=4)
                        nc.vector.tensor_scalar(zp[:, t.buf(4), 0, 0:D], one(xres, t), mv2[:, t.buf(2), 0:1],
                                                rs2[:, t.buf(2), :], ALU.subtract, ALU.mult).then_inc(zn_done, 1)
                    if t := ATTENTION.at(s, 0):
                        wait_for(dve, pv_ps, t)
                        wait_for(dve, oT_ps, t, back=2)
                        o = psO[0:S, 0:2 * OROW].rearrange("p (b c) -> p b c", b=2)[:, :, 0:PAIRS * VW] \
                            .rearrange("p b (h w) -> p b h w", w=DH + 1)
                        nc.vector.reciprocal(rden[:, :, :], o[:, :, :, DH]).then_inc(rden_done, 1)
                        wait_for(dve, rden_done, t)
                        for b in range(2):
                            nc.vector.tensor_tensor(on[b * S:(b + 1) * S, t.buf(2), :].rearrange("p (h w) -> p h w", w=DH),
                                                    o[:, b, :, 0:DH],
                                                    rden[:, b, :].unsqueeze(2).broadcast_to([S, H, DH]),
                                                    ALU.mult).then_inc(on_done, 1)

                ATTENTION.run(dve, step)

            @block.gpsimd
            def _(pool):
                nc.gpsimd.memset(ident[:, :], 0.0).then_inc(ident_ready, 1)
                pool.wait_ge(ident_ready, 1)
                nc.gpsimd.affine_select(out=ident[:, :], in_=ident[:, :], compare_op=ALU.not_equal, fill=1.0, base=0,
                                        pattern=[[-1, P]], channel_multiplier=1).then_inc(ident_ready, 1)
                nc.gpsimd.memset(allone[:, :], 1.0).then_inc(route_ready, 1)
                nc.gpsimd.memset(before[:, :, :, :], 0.0).then_inc(route_ready, 1)
                pool.wait_ge(route_ready, 2)
                pool.wait_ge(zero_ready, 4)
                pool.wait_ge(ones_ready, 1)
                pool.wait_ge(bias_ready, 1)

                nc.gpsimd.iota(iot[:, :], pattern=[[1, E]], base=0, channel_multiplier=0,
                               allow_small_or_imprecise_dtypes=True).then_inc(route_ready, 1)
                nc.gpsimd.iota(base[:, :], pattern=[[CAP, E]], base=0, channel_multiplier=0,
                               allow_small_or_imprecise_dtypes=True).then_inc(route_ready, 1)
                nc.gpsimd.iota(tokid[:, :, :], pattern=[[P, NT], [NT * P, 2]], base=0, channel_multiplier=1).then_inc(pad_ready, 1)
                nc.gpsimd.affine_select(out=lower[:, :], in_=allone[:, :], compare_op=ALU.is_gt, fill=0.0, base=0,
                                        pattern=[[1, P]], channel_multiplier=-1).then_inc(route_ready, 1)
                pool.wait_ge(pad_ready, 1)

                def step(s):
                    if t := ATTENTION.at(s, 2):
                        wait_for(pool, rope_done, t)
                        wait_for(pool, kT_ps, t, back=2)
                        wait_for(pool, v9_done, t, back=2, per=4)
                        nc.gpsimd.tensor_tensor(kvr[:, t.buf(2), :], ropA[:, t.buf(2), :], ropB[:, t.buf(2), :],
                                                ALU.add).then_inc(kvr_done, 1)
                    if (t := ATTENTION.at(s, 4)) and not t.buf(2):
                        r = slice(t.buf(4), t.buf(4) + 2)
                        wait_for(pool, mv1_done, t + 1)
                        wait_for(pool, xn_done, t, back=3)
                        carry(pool)
                        nc.gpsimd.tensor_scalar(ve1[:, r], mv1[:, r, 1], EPS, None, ALU.add).then_inc(ve1_done, 2)
                        wait_for(pool, ve1_done, t + 1)
                        nc.gpsimd.tensor_tensor(rs1[:, r], ve1[:, r], mhalf[:, :], ALU.pow).then_inc(rs1_done, 2)
                    if (t := ATTENTION.at(s, -2)) and t.buf(2):
                        q = t.buf(4) // 2
                        wait_for(pool, chosen_done, t)
                        wait_for(pool, before_done, t, back=2)
                        nc.gpsimd.tensor_tensor(before[:, q, 1, :], before[:, q, 0, :], chosen[:, q, 0, :], ALU.add).then_inc(before_done, 1)
                        wait_for(pool, before_done, t, back=1)
                        wait_for(pool, place_ps, t, back=2)
                        nc.gpsimd.tensor_tensor(before[:, 1 - q, 0, :], before[:, q, 1, :], chosen[:, q, 1, :], ALU.add).then_inc(before_done, 1)
                    if t := ATTENTION.at(s, -1):
                        wait_for(pool, mv2_done, t)
                        carry(pool)
                        nc.gpsimd.tensor_scalar(ve2[:, t.buf(2), :], mv2[:, t.buf(2), 1:2], EPS, None, ALU.add).then_inc(ve2_done, 1)
                        wait_for(pool, ve2_done, t)
                        wait_for(pool, zn_done, t, back=2)
                        nc.gpsimd.tensor_tensor(rs2[:, t.buf(2), :], ve2[:, t.buf(2), :], mhalf[:, 0:1], ALU.pow).then_inc(rs2_done, 1)
                    if t := ATTENTION.at(s, 3):
                        wait_for(pool, xn_done, t)
                        nc.gpsimd.tensor_tensor(one(xres, t), one(xres, t), bpg[:, :], ALU.add).then_inc(xb_done, 1)
                    if (t := ATTENTION.at(s, -3)) and t.buf(2):
                        r = slice(t.buf(4) - 1, t.buf(4) + 1)
                        src = tokid[:, t.val - 1:t.val + 1, :] if isinstance(t.val, int) else tokid[:, bass.ds(t.val - 1, 2), :]
                        for i in (1, 0):
                            wait_slot(pool, row_out, t + -i, 32, back=4)
                        carry(pool)
                        nc.gpsimd.tensor_copy(zp[:, r, :, D].bitcast(U32), src).then_inc(tok_done, 2)
                    if t := ATTENTION.at(s, -4):
                        pair = t + (0 if t.buf(2) else 1)
                        wait_for(pool, dest_done, pair)
                        wait_for(pool, weight_done, pair)
                        wait_for(pool, tok_done, pair)
                        wait_for(pool, z2_done, t)
                        carry(pool)
                        for j in range(2):
                            nc.gpsimd.indirect_dma_start(
                                A["lists"], bass.IndirectOffsetOnAxis(ap=dest[:, t.buf(4) // 2, t.buf(2), j:j + 1], axis=0),
                                zp[:, t.buf(4), j, :], None).then_inc(row_out[t.buf(4)], 16)

                ATTENTION.run(pool, step)

        pad = sb("pad", [P, ROW])
        cnt = sb("cnt", [P, E])
        ntu = sb("ntu", [P, 2, E], U32)
        ntf = sb("ntf", [P, E])
        upto = sb("upto", [P, E])
        jump = sb("jump", [P, E])
        zero8 = sb("zero8", [P, E])
        pcol = sb("pcol", [P, 1])
        padrow = sb("padrow", [P, E], U32)
        tile_no = sb("tile_no", [P, NET])
        past = sb("past", [P, NET, E])
        hop = sb("hop", [P, NET, E])
        tfl = sb("tfl", [P, 2, NET])
        first128 = sb("first128", [P, NET])
        table = sb("table", [P, 2, NET], U32)
        zin = sb("zin", [P, 8, ROW])
        zT = sb("zT", [P, 2, P])
        hs = sb("hs", [P, 2, HID])
        hm = sb("hm", [P, 2, HID])
        hT = sb("hT", [P, 2, 2, P])
        ys = sb("ys", [P, 8, D])
        psH, psT, psZ, psY = psS, psP, [psX, psK], [psO, psG]
        count_ps, table_step, filled, e_const = sem("count_ps"), sem("table_step"), sem("filled"), sem("e_const")
        ez_ps, ez_sb, h_ps, silu_done, h_done = sem("ez_ps"), sem("ez_sb"), sem("h_ps"), sem("silu_done"), sem("h_done")
        hT_ps, hT_sb, y_ps, y_sb = sem("hT_ps"), sem("hT_sb"), sem("y_ps"), sem("y_sb")
        z_in = [sem(f"z_in{i}") for i in range(8)]
        y_out = [sem(f"y_out{i}") for i in range(8)]
        lists, results = A["lists"], A["results"]

        with nc.Block() as block:
            @block.gpsimd
            def _(pool):
                nc.gpsimd.iota(tile_no[:, :], pattern=[[1, NET]], base=0, channel_multiplier=0,
                               allow_small_or_imprecise_dtypes=True).then_inc(e_const, 1)
                nc.gpsimd.iota(first128[:, :], pattern=[[P, NET]], base=0, channel_multiplier=0,
                               allow_small_or_imprecise_dtypes=True).then_inc(e_const, 1)
                nc.gpsimd.iota(pcol[:, :], pattern=[[0, 1]], base=0, channel_multiplier=1,
                               allow_small_or_imprecise_dtypes=True).then_inc(e_const, 1)
                nc.gpsimd.memset(pad[:, :], 0.0).then_inc(e_const, 1)
                pool.wait_ge(e_const, 4)
                nc.gpsimd.iota(pad[:, D:D + 1].bitcast(U32), pattern=[[0, 1]], base=NOWHERE, channel_multiplier=0).then_inc(e_const, 1)
                pool.wait_ge(e_const, 5)
                pool.wait_ge(table_step, 2)
                for e in range(E):
                    nc.gpsimd.indirect_dma_start(lists, bass.IndirectOffsetOnAxis(ap=padrow[:, e:e + 1], axis=0),
                                                 pad[:, :], None).then_inc(filled, 16)

                def step(s):
                    if t := EXPERTS.at(s, -2):
                        wait_for(pool, y_sb, t)
                        carry(pool)
                        nc.gpsimd.indirect_dma_start(
                            results, bass.IndirectOffsetOnAxis(ap=zin[:, t.buf(8), D:D + 1].bitcast(U32), axis=0),
                            ys[:, t.buf(8), :], None, bounds_check=NOWHERE - 1, oob_is_err=False).then_inc(y_out[t.buf(8)], 16)

                EXPERTS.run(pool, step)
                for n in y_out:
                    pool.wait_ge(n, 16 * (NET // 8))

            @block.sync
            def _(sp):
                sp.wait_ge(e_const, 5)
                for n in range(SPARE):
                    sp.dma_start(lists[E * CAP + n * P:E * CAP + (n + 1) * P, :], pad[:, :]).then_inc(spare_out, 16)
                for n in row_out:
                    sp.wait_ge(n, 32 * (NT // 4))
                sp.wait_ge(filled, 16 * E)
                sp.wait_ge(spare_out, 16 * SPARE)
                sp.wait_ge(table_step, 12)

                def load(t):
                    row = sp.value_load(table[0:1, 1, t.val:t.val + 1] if isinstance(t.val, int) else table[0:1, 1, bass.ds(t.val, 1)],
                                        min_val=0, max_val=ZROWS - P)
                    wait_slot(sp, y_out, t, 16, back=8)
                    carry(sp)
                    sp.dma_start(zin[:, t.buf(8), :], lists[bass.ds(row, P), :]).then_inc(z_in[t.buf(8)], 16)

                for t in range(8):
                    load(Tile(8, None, t))
                with sp.Fori(1, NET // 8) as turn:
                    for u in range(8):
                        load(Tile(8, turn, u))

            @block.tensor
            def _(pe):
                pe.matmul(psG[:, 0:E], allone[:, :], before[:, 0, 0, :], start=True, stop=True).then_inc(count_ps, 1)
                pe.wait_ge(experts_in, 16 * (2 + E))
                pe.wait_ge(table_step, 12)

                def expert(t):
                    return pe.value_load(table[0:1, 0, t.val:t.val + 1] if isinstance(t.val, int) else table[0:1, 0, bass.ds(t.val, 1)],
                                         min_val=0, max_val=E - 1)

                def step(s):
                    if t := EXPERTS.at(s, 1):
                        e = expert(t)
                        wait_for(pe, ez_sb, t)
                        wait_for(pe, h_done, t, back=2)
                        pe.matmul(psH[t.buf(2)][:, :], zT[:, t.buf(2), :], w01[:, bass.ds(e, 1), :, :].rearrange("p o a h -> p (o a h)"),
                                  start=True, stop=True).then_inc(h_ps, 1)
                    if t := EXPERTS.at(s, 0):
                        wait_for(pe, h_done, t)
                        wait_for(pe, hT_sb, t, back=2)
                        for k in range(2):
                            last = pe.transpose(psT[t.buf(2)][:, k * P:(k + 1) * P], hm[:, t.buf(2), k * P:(k + 1) * P], ident[:, :])
                        last.then_inc(hT_ps, 1)
                    if t := EXPERTS.at(s, 2):
                        wait_slot(pe, z_in, t, 16)
                        wait_for(pe, ez_sb, t, back=2)
                        pe.transpose(psZ[t.buf(2)][:, 0:P], zin[:, t.buf(8), 0:D], ident[:, :]).then_inc(ez_ps, 1)
                    if t := EXPERTS.at(s, -1):
                        e = expert(t)
                        wait_for(pe, hT_sb, t)
                        wait_for(pe, y_sb, t, back=2)
                        for k in range(2):
                            last = pe.matmul(psY[t.buf(2)][:, 0:D], hT[:, t.buf(2), k, :], wo[:, bass.ds(e, 1), k, :].squeeze(1),
                                             start=(k == 0), stop=(k == 1))
                        last.then_inc(y_ps, 1)

                EXPERTS.run(pe, step)

            @block.scalar
            def _(act):
                act.wait_ge(table_step, 12)

                def step(s):
                    if t := EXPERTS.at(s, 0):
                        wait_for(act, hT_ps, t)
                        wait_for(act, y_ps, t, back=2)
                        nc.scalar.copy(hT[:, t.buf(2), :, :], psT[t.buf(2)][:, 0:2 * P].rearrange("p (k c) -> p k c", k=2)).then_inc(hT_sb, 1)
                    if t := EXPERTS.at(s, 1):
                        wait_for(act, h_ps, t)
                        wait_for(act, h_done, t, back=2)
                        nc.scalar.activation(hs[:, t.buf(2), :], psH[t.buf(2)][:, 0:HID], ACT.Silu).then_inc(silu_done, 1)
                    if t := EXPERTS.at(s, -1):
                        wait_for(act, y_ps, t)
                        wait_slot(act, y_out, t, 16, back=8)
                        nc.scalar.activation(ys[:, t.buf(8), :], psY[t.buf(2)][:, 0:D], ACT.Copy,
                                             scale=zin[:, t.buf(8), D + 1:D + 2]).then_inc(y_sb, 1)

                EXPERTS.run(act, step)

            @block.vector
            def _(dve):
                n = [0]

                def then(ins):
                    n[0] += 1
                    ins.then_inc(table_step, 1)
                    dve.wait_ge(table_step, n[0])

                dve.wait_ge(e_const, 5)
                dve.wait_ge(count_ps, 1)
                then(nc.vector.tensor_copy(cnt[:, :], psG[:, 0:E]))
                then(nc.vector.scalar_tensor_tensor(out=padrow[:, :], in0=cnt[:, :], scalar=pcol[:, 0:1], in1=base[:, :],
                                                    op0=ALU.add, op1=ALU.add))
                then(nc.vector.tensor_scalar(ntu[:, 0, :], cnt[:, :], float(P - 1), None, ALU.add))
                then(nc.vector.tensor_scalar(ntu[:, 1, :], ntu[:, 0, :], 7, None, ALU.logical_shift_right))
                then(nc.vector.tensor_copy(ntf[:, :], ntu[:, 1, :]))
                nc.vector.memset(zero8[:, :], 0.0)
                then(nc.vector.tensor_scalar(jump[:, :], ntf[:, :], -float(P), float(CAP), ALU.mult, ALU.add))
                then(nc.vector.tensor_tensor_scan(upto[:, :], ntf[:, :], zero8[:, :], 0.0, ALU.add, ALU.add))
                then(nc.vector.tensor_tensor(past[:, :, :], upto[:, :].unsqueeze(1).broadcast_to([P, NET, E]),
                                             tile_no[:, :].unsqueeze(2).broadcast_to([P, NET, E]), ALU.is_le))
                nc.vector.tensor_reduce(tfl[:, 0, :], past[:, :, :], AX_X, ALU.add)
                then(nc.vector.tensor_tensor(hop[:, :, :], past[:, :, :], jump[:, :].unsqueeze(1).broadcast_to([P, NET, E]), ALU.mult))
                then(nc.vector.tensor_reduce(tfl[:, 1, :], hop[:, :, :], AX_X, ALU.add))
                then(nc.vector.tensor_scalar(table[:, 0, :], tfl[:, 0, :], float(E - 1), None, ALU.min))
                then(nc.vector.tensor_tensor(table[:, 1, :], tfl[:, 1, :], first128[:, :], ALU.add))

                def step(s):
                    if t := EXPERTS.at(s, 2):
                        wait_for(dve, ez_ps, t)
                        wait_for(dve, h_ps, t, back=2)
                        nc.vector.tensor_copy(zT[:, t.buf(2), :], psZ[t.buf(2)][:, 0:P]).then_inc(ez_sb, 1)
                    if t := EXPERTS.at(s, 1):
                        wait_for(dve, silu_done, t)
                        wait_for(dve, hT_ps, t, back=2)
                        nc.vector.tensor_tensor(hm[:, t.buf(2), :], psH[t.buf(2)][:, HID:2 * HID], hs[:, t.buf(2), :],
                                                ALU.mult).then_inc(h_done, 1)

                EXPERTS.run(dve, step)

        ya, yb = sb("ya", [P, 4, CHUNK, D]), sb("yb", [P, 4, CHUNK, D])
        y_in = [sem(f"y_in{i}") for i in range(4)]
        sum_done, total_done, out_done = sem("sum_done"), sem("total_done"), sem("out_done")
        r_d = results.rearrange("(j c i p) d -> j p c i d", j=2, i=CHUNK, p=P)
        xr_c = xres[:, :, :].rearrange("p (c i) d -> p c i d", i=CHUNK)
        o_c = o_d.rearrange("p (c i) d -> p c i d", i=CHUNK)

        with nc.Block() as block:
            @block.sync
            def _(sp):
                def step(s):
                    if t := COMBINE.at(s, 0):
                        wait_for(sp, total_done, t, back=4)
                        carry(sp)
                        for y, j in ((ya, 0), (yb, 1)):
                            sp.dma_start(y[:, t.buf(4), :, :], r_d[j][:, bass.ds(t.val, 1), :, :].squeeze(1)).then_inc(y_in[t.buf(4)], 16)

                COMBINE.run(sp, step)

            @block.vector
            def _(dve):
                def step(s):
                    if t := COMBINE.at(s, 0):
                        wait_slot(dve, y_in, t, 32)
                        nc.vector.tensor_tensor(ya[:, t.buf(4), :, :], ya[:, t.buf(4), :, :], yb[:, t.buf(4), :, :], ALU.add).then_inc(sum_done, 1)
                        wait_for(dve, sum_done, t)
                        x1 = xr_c[:, bass.ds(t.val, 1), :, :].squeeze(1)
                        nc.vector.tensor_tensor(x1, x1, ya[:, t.buf(4), :, :], ALU.add).then_inc(total_done, 1)

                COMBINE.run(dve, step)

            @block.scalar
            def _(act):
                def step(s):
                    if t := COMBINE.at(s, 0):
                        wait_for(act, total_done, t)
                        act.dma_start(o_c[:, bass.ds(t.val, 1), :, :].squeeze(1), xr_c[:, bass.ds(t.val, 1), :, :].squeeze(1)).then_inc(out_done, 16)

                COMBINE.run(act, step)
                act.wait_ge(out_done, 16 * (NT // CHUNK))


_INS = ["x", "ctx_1024", "g_xattn", "g_ffn", "L0_xattn_Wq", "L0_xattn_Wk", "L0_xattn_Wv", "L0_xattn_Wp", "L0_xattn_bp",
        "L0_ffn_gate_kernel", "L0_ffn_w0_kernel", "L0_ffn_w1_kernel", "L0_ffn_wo_kernel"]


def shape_constants():
    import numpy as np
    theta = (np.float32(1.0) / np.float32(10000.0) ** (np.float32(2.0) * np.arange(D // 2, dtype=np.float32) / np.float32(D))).astype(np.float32)
    ang = np.arange(S, dtype=np.float32)[:, None] * theta[None, :]
    cos, sin = np.cos(ang), np.sin(ang)
    cos2 = np.repeat(cos, 2, axis=1)
    sin2 = np.stack([-sin, sin], axis=-1).reshape(S, D)
    mask = (np.arange(D)[:, None] // DH % 4 == np.arange(4)[None, :])
    return {"rope_cos": np.tile(cos2, (P // S, 1)).astype(np.float32), "rope_sin": np.tile(sin2, (P // S, 1)).astype(np.float32),
            "head_mask": mask.astype(np.float32)}


def kernel(**inputs):
    import numpy as _np
    import concourse.bacc as _bacc
    from concourse import mybir as _mybir
    from concourse.bass_utils import run_bass_kernel_spmd as _run

    nc = _bacc.Bacc("TRN2", target_bir_lowering=False, num_devices=1)
    arrays, args = {}, {}
    for name, a in [(n, inputs[n]) for n in _INS] + list(shape_constants().items()):
        a = _np.ascontiguousarray(a)
        arrays[f"in_{name}_dram"] = a
        args[name] = nc.dram_tensor(f"in_{name}_dram", a.shape, _mybir.dt.from_np(a.dtype), kind="ExternalInput").ap()
    args["lists"] = nc.dram_tensor("lists", (ZROWS, ROW), F32, kind="Internal").ap()
    args["results"] = nc.dram_tensor("results", (2 * NT * P, D), F32, kind="Internal").ap()
    out = nc.dram_tensor("out_0_dram", (NB, S, D), F32, kind="ExternalOutput").ap()
    flamingo_block(nc, args, out)
    r = _run(nc, [arrays], core_ids=[0])
    return r.results[0]["out_0_dram"]
```

```python
from contextlib import ExitStack

import concourse.bass as bass
from concourse import mybir

F32 = mybir.dt.float32
BF16 = mybir.dt.bfloat16
F32R = mybir.dt.float32r
U32 = mybir.dt.uint32
ALU = mybir.AluOpType
ACT = mybir.ActivationFunctionType
AX_X = mybir.AxisListType.X

P = 128
NB, S, D = 128, 64, 128
H, DH = 16, 8
NT = NB * S // P
PAIRS = H // 2
E, HID = 8, 256
ET = 2 * P
CAP = NT * P + ET
SPARE = E
ZROWS = E * CAP + SPARE * ET
ROW = D + 2
NET = 2 * NT * P // ET + E
NOWHERE = 2 * NT * P
EPS = 1e-5
SCALE = float(DH) ** -0.5
VW = 2 * (DH + 1)
VPAD = 64
VROW = (PAIRS - 1) * VW + VPAD
OROW = 192


class Tile:

    def __init__(self, unroll, turn, k):
        self.unroll, self.turn, self.k = unroll, turn, k
        self.val = k if turn is None else unroll * turn + k

    @property
    def lap(self):
        return self.k // self.unroll + (0 if self.turn is None else self.turn)

    def buf(self, n):
        return self.k % n

    def __add__(self, n):
        return Tile(self.unroll, self.turn, self.k + n)


class Pipeline:

    def __init__(self, tiles, behind, ahead, unroll, steady):
        self.tiles, self.unroll, self.steady = tiles, unroll, steady
        self.first, self.last = -ahead, tiles - 1 + behind
        self.turns = (tiles - ahead - steady) // unroll

    def at(self, step, off):
        turn, u = step
        if turn is None:
            return Tile(self.unroll, None, u + off) if 0 <= u + off < self.tiles else None
        return Tile(self.unroll, turn, self.steady + u + off)

    def run(self, eng, body):
        for t in range(self.first, self.steady):
            body((None, t))
        with eng.Fori(0, self.turns) as turn:
            for u in range(self.unroll):
                body((turn, u))
        for t in range(self.steady + self.unroll * self.turns, self.last + 1):
            body((None, t))


ATTENTION = Pipeline(NT, behind=4, ahead=4, unroll=4, steady=9)
EXPERTS = Pipeline(NET, behind=1, ahead=2, unroll=8, steady=10)
CHUNK = 4
COMBINE = Pipeline(NT // CHUNK, behind=0, ahead=0, unroll=4, steady=4)


def wait_for(eng, sem, t, back=0, per=1, part=None):
    v = per * (t.val - back) + (per if part is None else part + 1)
    if isinstance(v, int) and v <= 0:
        return
    eng.wait_ge(sem, v)


def wait_slot(eng, sems, t, per, back=0):
    v = per * (t.lap + 1 - back // t.unroll)
    if isinstance(v, int) and v <= 0:
        return
    eng.wait_ge(sems[t.buf(t.unroll)], v)


def carry(eng):
    eng.nop(nofuse=True)


def flamingo_block(nc, A, out):
    with ExitStack() as ctx:
        def sb(name, shape, dt=F32):
            return ctx.enter_context(nc.sbuf_tensor(name, shape, dt))

        def ps(name):
            return ctx.enter_context(nc.psum_tensor(name, [P, 512], F32))

        def sem(name):
            return ctx.enter_context(nc.semaphore(name))

        xres = sb("xres", [P, NT, D])
        cring = sb("cring", [P, 4, D])
        ident = sb("ident", [P, P])
        minus = sb("minus", [P, P], F32R)
        wnat = sb("wnat", [P, 4, D])
        wT = sb("wT", [P, 4, D])
        wperm = sb("wperm", [P, D])
        cosT = sb("cosT", [P, D])
        sinT = sb("sinT", [P, D])
        hmask = sb("hmask", [P, 4])
        gcol = sb("gcol", [P, 2])
        tg = sb("tg", [P, 2])
        bp = sb("bp", [P, D])
        bpg = sb("bpg", [P, D])
        mhalf = sb("mhalf", [P, 2])
        gatew = sb("gatew", [P, D])
        w01 = sb("w01", [P, E, 2, HID])
        wo = sb("wo", [P, E, 2, D])
        st1, st2 = sb("st1", [P, 2, 6]), sb("st2", [P, 2, 6])
        mv1, mv2 = sb("mv1", [P, 4, 2]), sb("mv2", [P, 2, 2])
        ve1, ve2 = sb("ve1", [P, 4]), sb("ve2", [P, 2, 1])
        rs1, rs2 = sb("rs1", [P, 4]), sb("rs2", [P, 2, 1])
        xn = sb("xn", [P, 2, D])
        xcT = sb("xcT", [P, 2, 2 * D])
        ropA = sb("ropA", [P, 2, 2 * D])
        ropB = sb("ropB", [P, 2, 2 * D])
        kvr = sb("kvr", [P, 2, 2 * D])
        qblk = sb("qblk", [P, 2, 2, 4, S])
        kfull = sb("kfull", [P, 2, 4, D])
        v9 = sb("v9", [P, 4, 2, VROW])
        ex = sb("ex", [P, 2, 2, 512])
        mx = sb("mx", [P, 2, PAIRS], F32R)
        pT = sb("pT", [P, 2, 2, 512])
        rden = sb("rden", [S, 2, 2 * PAIRS])
        on = sb("on", [P, 2, D])
        oT = sb("oT", [P, 2, D])
        zp = sb("zp", [P, 4, 2, ROW])
        zTs = sb("zTs", [P, 2, D])
        top = sb("top", [P, 4, 8])
        idx = sb("idx", [P, 4, 8], U32)
        idf = sb("idf", [P, 2, 2, 2])
        gap = sb("gap", [P, 2, 2])
        egap = sb("egap", [P, 2, 2])
        den2 = sb("den2", [P, 2])
        rden2 = sb("rden2", [P, 2])
        iot = sb("iot", [P, E])
        base = sb("base", [P, E])
        oh = sb("oh", [P, 2, 2, 2, E])
        chosen = sb("chosen", [P, 2, 2, E], BF16)
        before = sb("before", [P, 2, 2, E], BF16)
        place = sb("place", [P, 2, E])
        hit = sb("hit", [P, 2, 2, E])
        dest = sb("dest", [P, 2, 2, 2], U32)
        tokid = sb("tokid", [P, NT, 2], U32)
        lower = sb("lower", [P, P], BF16)
        allone = sb("allone", [P, P], BF16)

        psS = [ps("psS0"), ps("psS1")]
        psP = [ps("psP0"), ps("psP1")]
        psX = ps("psX")
        psK = ps("psK")
        psO = ps("psO")
        psG = ps("psG")

        weights_in, experts_in, tiles_in = sem("weights_in"), sem("experts_in"), sem("tiles_in")
        ident_ready, zero_ready, ones_ready = sem("ident_ready"), sem("zero_ready"), sem("ones_ready")
        wp_ready, minus_ready = sem("wp_ready"), sem("minus_ready")
        wT_ps, wT_sb, tanh_ready, bias_ready = sem("wT_ps"), sem("wT_sb"), sem("tanh_ready"), sem("bias_ready")
        st1_done, mv1_done, ve1_done, rs1_done = sem("st1_done"), sem("mv1_done"), sem("ve1_done"), sem("rs1_done")
        xn_done, xb_done, xc_ps, xc_sb = sem("xn_done"), sem("xb_done"), sem("xc_ps"), sem("xc_sb")
        q_ps, kv_ps, q_sb, rope_done = sem("q_ps"), sem("kv_ps"), sem("q_sb"), sem("rope_done")
        v9_done, kT_ps, kT_sb = sem("v9_done"), sem("kT_ps"), sem("kT_sb")
        s_ps, mx_done, shift_ps, exp_done = sem("s_ps"), sem("mx_done"), sem("shift_ps"), sem("exp_done")
        p_ps, p_sb, pv_ps, rden_done, on_done = sem("p_ps"), sem("p_sb"), sem("pv_ps"), sem("rden_done"), sem("on_done")
        oT_ps, oT_sb, attn_ps, x1_done = sem("oT_ps"), sem("oT_sb"), sem("attn_ps"), sem("x1_done")
        st2_done, mv2_done, ve2_done, rs2_done = sem("st2_done"), sem("mv2_done"), sem("ve2_done"), sem("rs2_done")
        zn_done, z_ps, z_sb, lg_ps, lg_sb = sem("zn_done"), sem("z_ps"), sem("z_sb"), sem("lg_ps"), sem("lg_sb")
        kvr_done, z2_done, top_done, idf_done = sem("kvr_done"), sem("z2_done"), sem("top_done"), sem("idf_done")
        oh_done, gap_done, egap_done, chosen_done = sem("oh_done"), sem("gap_done"), sem("egap_done"), sem("chosen_done")
        before_done, place_ps, den2_done, rden2_done = sem("before_done"), sem("place_ps"), sem("den2_done"), sem("rden2_done")
        weight_done, place_done, hit_done, dest_done = sem("weight_done"), sem("place_done"), sem("hit_done"), sem("dest_done")
        tok_done, route_ready, pad_ready, spare_out = sem("tok_done"), sem("route_ready"), sem("pad_ready"), sem("spare_out")
        row_out = [sem(f"row_out{i}") for i in range(4)]

        pad = sb("pad", [P, 2, ROW])
        cnt = sb("cnt", [P, E])
        ntu = sb("ntu", [P, 2, E], U32)
        ntf = sb("ntf", [P, E])
        upto = sb("upto", [P, E])
        jump = sb("jump", [P, E])
        zero8 = sb("zero8", [P, E])
        padrow = sb("padrow", [P, E], U32)
        tile_no = sb("tile_no", [P, NET])
        past = sb("past", [P, NET, E])
        hop = sb("hop", [P, NET, E])
        tfl = sb("tfl", [P, 2, NET])
        first_row = sb("first_row", [P, NET])
        table = sb("table", [P, 2, NET], U32)
        warm = sb("warm", [P, 1])
        zin = sb("zin", [P, 8, 2, ROW])
        zT = sb("zT", [P, 2, ET])
        wcur = sb("wcur", [P, 2, 2, HID])
        hs = sb("hs", [P, 2, 2 * ET])
        hm = sb("hm", [P, 2, 2, ET])
        ys = sb("ys", [P, 8, 2, D])
        psA, psB, psZ, psY = psS, psP, [psX, psK], [psO, psG]
        count_ps, table_step, filled, e_const = sem("count_ps"), sem("table_step"), sem("filled"), sem("e_const")
        ez_ps, ez_sb, a_ps, b_ps, silu_done, h_done = sem("ez_ps"), sem("ez_sb"), sem("a_ps"), sem("b_ps"), sem("silu_done"), sem("h_done")
        y_ps, y_sb, warm_done, w_done = sem("y_ps"), sem("y_sb"), sem("warm_done"), sem("w_done")
        z_in = [sem(f"z_in{i}") for i in range(8)]
        y_out = [sem(f"y_out{i}") for i in range(8)]
        lists, results = A["lists"], A["results"]

        x_d = A["x"].rearrange("b s d -> (b s) d").rearrange("(t p) d -> p t d", p=P)
        c_d = A["ctx_1024"].rearrange("b s d -> (b s) d").rearrange("(t p) d -> p t d", p=P)
        o_d = out.rearrange("b s d -> (b s) d").rearrange("(t p) d -> p t d", p=P)

        def one(ap, t):
            return ap[:, t.val, :] if isinstance(t.val, int) else ap[:, bass.ds(t.val, 1), :].squeeze(1)

        def pad_list(eng, e):
            row = eng.value_load(padrow[0:1, e:e + 1], min_val=0, max_val=ZROWS - ET)
            eng.dma_start(lists[bass.ds(row, ET), :].rearrange("(p h) c -> p h c", h=2), pad[:, :, :]).then_inc(filled, 16)

        def expert(eng, t):
            return eng.value_load(table[0:1, 0, t.val:t.val + 1] if isinstance(t.val, int) else table[0:1, 0, bass.ds(t.val, 1)],
                                  min_val=0, max_val=E - 1)

        yy = sb("yy", [P, 4, CHUNK, 2, D])
        y_in = [sem(f"y_in{i}") for i in range(4)]
        sum_done, total_done, out_done = sem("sum_done"), sem("total_done"), sem("out_done")
        r_d = results.rearrange("(c i p j) d -> p c i (j d)", j=2, i=CHUNK, p=P)
        xr_c = xres[:, :, :].rearrange("p (c i) d -> p c i d", i=CHUNK)
        o_c = o_d.rearrange("p (c i) d -> p c i d", i=CHUNK)

        with nc.Block() as block:
            @block.sync
            def _(sp):
                def load(t):
                    wait_for(sp, tiles_in, t, back=1, per=32)
                    carry(sp)
                    wait_for(sp, xc_ps, t, back=4)
                    carry(sp)
                    sp.dma_start(one(xres, t), one(x_d, t)).then_inc(tiles_in, 16)
                    sp.dma_start(cring[:, t.buf(4), :], one(c_d, t)).then_inc(tiles_in, 16)

                load(Tile(4, None, 0))
                for n, w in enumerate(("L0_xattn_Wq", "L0_xattn_Wk", "L0_xattn_Wv", "L0_xattn_Wp")):
                    sp.dma_start(wnat[:, n, :], A[w]).then_inc(weights_in, 16)
                load(Tile(4, None, 1))
                sp.wait_ge(zero_ready, 4)
                sp.dma_start(gatew[:, 0:E], A["L0_ffn_gate_kernel"]).then_inc(weights_in, 16)
                for t in range(2, 4):
                    load(Tile(4, None, t))
                with sp.Fori(1, NT // 4) as turn:
                    for u in range(4):
                        load(Tile(4, turn, u))
                sp.dma_start(w01[:, :, 0, :], A["L0_ffn_w0_kernel"].rearrange("e d h -> d e h")).then_inc(experts_in, 16)
                sp.dma_start(w01[:, :, 1, :], A["L0_ffn_w1_kernel"].rearrange("e d h -> d e h")).then_inc(experts_in, 16)
                for e in range(E):
                    sp.dma_start(wo[:, e, :, :], A["L0_ffn_wo_kernel"][e].rearrange("(k h) d -> h k d", k=2)).then_inc(experts_in, 16)
                sp.wait_ge(e_const, 5)
                for n in range(SPARE):
                    sp.dma_start(lists[E * CAP + n * ET:E * CAP + (n + 1) * ET, :].rearrange("(p h) c -> p h c", h=2), pad[:, :, :]).then_inc(spare_out, 16)

                sp.wait_ge(table_step, 2)
                for e in range(0, E, 2):
                    pad_list(sp, e)
                for n in row_out:
                    sp.wait_ge(n, 32 * (NT // 4))
                sp.wait_ge(filled, 16 * E)
                sp.wait_ge(spare_out, 16 * SPARE)
                sp.wait_ge(table_step, 12)

                def load(t):
                    row = sp.value_load(table[0:1, 1, t.val:t.val + 1] if isinstance(t.val, int) else table[0:1, 1, bass.ds(t.val, 1)],
                                        min_val=0, max_val=ZROWS - ET)
                    wait_slot(sp, y_out, t, 32, back=8)
                    carry(sp)
                    sp.dma_start(zin[:, t.buf(8), :, :], lists[bass.ds(row, ET), :].rearrange("(p h) c -> p h c", h=2)).then_inc(z_in[t.buf(8)], 16)

                for t in range(8):
                    load(Tile(8, None, t))
                with sp.Fori(1, NET // 8) as turn:
                    for u in range(8):
                        load(Tile(8, turn, u))

                for n in y_out:
                    sp.wait_ge(n, 32 * (NET // 8))

                def combine_step(s):
                    if t := COMBINE.at(s, 0):
                        wait_for(sp, total_done, t, back=4)
                        carry(sp)
                        sp.dma_start(yy[:, t.buf(4), :, :, :].rearrange("p i j d -> p i (j d)"),
                                     r_d[:, bass.ds(t.val, 1), :, :].squeeze(1)).then_inc(y_in[t.buf(4)], 16)

                COMBINE.run(sp, combine_step)

            @block.tensor
            def _(pe):
                pe.wait_ge(weights_in, 16 * 11)
                pe.wait_ge(ident_ready, 2)
                pe.wait_ge(wp_ready, 2)
                for n in range(4):
                    last = pe.transpose(psS[0][:, n * D:(n + 1) * D], wnat[:, n, :] if n < 3 else wperm[:, :], ident[:, :])
                last.then_inc(wT_ps, 1)
                pe.wait_ge(wT_sb, 2)
                pe.wait_ge(ones_ready, 1)
                pe.wait_ge(minus_ready, 1)
                pe.wait_ge(route_ready, 5)

                def attention_step(s):
                    def scores(b):
                        if t := ATTENTION.at(s, 1):
                            if b == 0:
                                wait_for(pe, kT_sb, t)
                                wait_for(pe, q_sb, t)
                            wait_for(pe, exp_done, t, back=1, per=2, part=b)
                            for jp in range(2):
                                last = pe.matmul(psS[b][:, jp * 256:(jp + 1) * 256],
                                                 qblk[:, t.buf(2), b, 2 * jp:2 * jp + 2, :].rearrange("p j q -> p (j q)"),
                                                 kfull[:, t.buf(2), :, b * S:(b + 1) * S], start=(jp == 0), stop=False,
                                                 skip_group_check=True)
                            last.then_inc(s_ps, 1)

                    def shift(b):
                        if t := ATTENTION.at(s, 1):
                            wait_for(pe, mx_done, t, per=2, part=b)
                            pe.matmul(psS[b][:, :], minus[:, :], mx[:, b, :].unsqueeze(2).broadcast_to([P, PAIRS, S]),
                                      start=False, stop=True, skip_group_check=True).then_inc(shift_ps, 1)

                    def attend(b):
                        if t := ATTENTION.at(s, 0):
                            if b == 0:
                                wait_for(pe, v9_done, t, per=4)
                                wait_for(pe, oT_sb, t, back=1)
                            wait_for(pe, p_sb, t, per=2, part=b)
                            for n in range(PAIRS):
                                g, jp, hp = n // 4, n // 2 % 2, n % 2
                                o = (2 * jp + g) * P + hp * S
                                last = pe.matmul(psO[0:S, b * OROW + n * VW:b * OROW + n * VW + VPAD],
                                                 pT[:, t.buf(2), b, o:o + S],
                                                 v9[:, t.buf(4), b, n * VW:n * VW + VPAD], start=True, stop=True)
                            if b == 1:
                                last.then_inc(pv_ps, 1)

                    scores(0)
                    if t := ATTENTION.at(s, -2):
                        wait_for(pe, zn_done, t)
                        wait_for(pe, lg_sb, t, back=1)
                        if n := ATTENTION.at(s, -1):
                            wait_for(pe, x1_done, n, back=1)
                        if (n := ATTENTION.at(s, -3)) and n.buf(2):
                            wait_for(pe, place_done, n)
                        pe.transpose(psG[:, P:2 * P], zp[:, t.buf(4), 0, 0:D], ident[:, :]).then_inc(z_ps, 1)
                    if t := ATTENTION.at(s, -1):
                        wait_for(pe, on_done, t, per=2)
                        pe.transpose(psO[:, 384:512], on[:, t.buf(2), :], ident[:, :]).then_inc(oT_ps, 1)
                    scores(1)
                    if t := ATTENTION.at(s, -2):
                        wait_for(pe, z_sb, t)
                        pe.matmul(psG[:, 256:384], zTs[:, t.buf(2), :], gatew[:, :], start=True, stop=True).then_inc(lg_ps, 1)
                    if t := ATTENTION.at(s, -1):
                        wait_for(pe, oT_sb, t)
                        pe.matmul(psG[:, 0:D], oT[:, t.buf(2), :], wT[:, 3, :], start=True, stop=True).then_inc(attn_ps, 1)
                    if t := ATTENTION.at(s, 0):
                        for b in range(2):
                            wait_for(pe, exp_done, t, per=2, part=b)
                            wait_for(pe, p_sb, t, back=1, per=2, part=b)
                            for n in range(4):
                                last = pe.transpose(psP[b][:, n * P:(n + 1) * P],
                                                    ex[:, t.buf(2), b, n * P:(n + 1) * P], ident[:, :])
                            last.then_inc(p_ps, 1)
                    if t := ATTENTION.at(s, 2):
                        wait_for(pe, kvr_done, t)
                        pe.transpose(psK[:, 256:384], kvr[:, t.buf(2), 0:D], ident[:, :]).then_inc(kT_ps, 1)
                    shift(0)
                    if t := ATTENTION.at(s, 3):
                        wait_for(pe, xn_done, t)
                        wait_for(pe, tiles_in, t, per=32)
                        wait_for(pe, q_sb, t, back=1)
                        pe.transpose(psX[:, 0:P], xn[:, t.buf(2), :], ident[:, :])
                        pe.transpose(psX[:, P:2 * P], cring[:, t.buf(4), :], ident[:, :]).then_inc(xc_ps, 1)
                    attend(0)
                    shift(1)
                    attend(1)
                    if t := ATTENTION.at(s, 3):
                        wait_for(pe, xc_sb, t)
                        pe.matmul(psX[:, 2 * P:3 * P], wT[:, 0, :], xcT[:, t.buf(2), 0:P], start=True, stop=True).then_inc(q_ps, 1)
                        wait_for(pe, kT_sb, t, back=1)
                        pe.matmul(psK[:, 0:2 * D], xcT[:, t.buf(2), P:2 * P], wT[:, 1:3, :], start=True, stop=True).then_inc(kv_ps, 1)
                    if (t := ATTENTION.at(s, -2)) and t.buf(2):
                        q = t.buf(4) // 2
                        wait_for(pe, chosen_done, t)
                        wait_for(pe, before_done, t)
                        if n := ATTENTION.at(s, -1):
                            wait_for(pe, x1_done, n)
                        pe.matmul(psG[:, 384:384 + 2 * E], lower[:, :], chosen[:, q, :, :], start=True, stop=False)
                        pe.matmul(psG[:, 384:384 + 2 * E], allone[:, :], before[:, q, :, :], start=False, stop=True).then_inc(place_ps, 2)

                ATTENTION.run(pe, attention_step)

                pe.wait_ge(before_done, NT)
                for n in (place_done, lg_sb, x1_done):
                    pe.wait_ge(n, NT)
                pe.matmul(psG[:, 0:E], allone[:, :], before[:, 0, 0, :], start=True, stop=True).then_inc(count_ps, 1)
                pe.wait_ge(experts_in, 16 * (2 + E))
                pe.wait_ge(table_step, 12)
                for n, per in ((exp_done, 2), (p_sb, 2), (q_sb, 1), (kT_sb, 1), (oT_sb, 1)):
                    pe.wait_ge(n, per * NT)

                def experts_step(s):
                    if t := EXPERTS.at(s, 2):
                        wait_slot(pe, z_in, t, 16)
                        wait_for(pe, ez_sb, t, back=2)
                        for h in range(2):
                            last = pe.transpose(psZ[t.buf(2)][:, h * P:(h + 1) * P], zin[:, t.buf(8), h, 0:D], ident[:, :])
                        last.then_inc(ez_ps, 1)
                    if t := EXPERTS.at(s, 1):
                        wait_for(pe, w_done, t)
                        wait_for(pe, ez_sb, t)
                        wait_for(pe, h_done, t, back=2)
                        for a, (bank, done) in enumerate(((psA, a_ps), (psB, b_ps))):
                            for k in range(2):
                                last = pe.matmul(bank[t.buf(2)][:, k * ET:(k + 1) * ET],
                                                 wcur[:, t.buf(2), a, k * P:(k + 1) * P],
                                                 zT[:, t.buf(2), :], start=True, stop=True)
                            last.then_inc(done, 1)
                    if t := EXPERTS.at(s, 0):
                        e = expert(pe, t)
                        wait_for(pe, h_done, t)
                        wait_for(pe, y_sb, t, back=2)
                        for h in range(2):
                            for k in range(2):
                                last = pe.matmul(psY[t.buf(2)][:, h * D:(h + 1) * D], hm[:, t.buf(2), k, h * P:(h + 1) * P],
                                                 wo[:, bass.ds(e, 1), k, :].squeeze(1), start=(k == 0), stop=(k == 1))
                        last.then_inc(y_ps, 1)

                EXPERTS.run(pe, experts_step)

            @block.scalar
            def _(act):
                act.dma_start(gcol[:, 0:1], A["g_xattn"].unsqueeze(0).broadcast_to([P, 1])).then_inc(weights_in, 16)
                act.dma_start(gcol[:, 1:2], A["g_ffn"].unsqueeze(0).broadcast_to([P, 1])).then_inc(weights_in, 16)
                act.dma_start(bp[:, :], A["L0_xattn_bp"].unsqueeze(0).broadcast_to([P, D])).then_inc(weights_in, 16)
                act.dma_start(cosT[:, :], A["rope_cos"]).then_inc(weights_in, 16)
                act.dma_start(sinT[:, :], A["rope_sin"]).then_inc(weights_in, 16)
                act.dma_start(hmask[:, :], A["head_mask"]).then_inc(weights_in, 16)
                act.wait_ge(weights_in, 16 * 11)
                nc.scalar.activation(tg[:, :], gcol[:, :], ACT.Tanh).then_inc(tanh_ready, 1)
                act.wait_ge(wT_ps, 1)
                nc.scalar.copy(wT[:, 0:3, :], psS[0][:, 0:3 * D].rearrange("p (a b) -> p a b", a=3)).then_inc(wT_sb, 1)
                act.wait_ge(tanh_ready, 1)
                nc.scalar.activation(wT[:, 3, :], psS[0][:, 3 * D:4 * D], ACT.Copy, scale=tg[:, 0:1]).then_inc(wT_sb, 1)
                act.wait_ge(zero_ready, 4)

                def attention_step(s):
                    def exponentials(b):
                        if t := ATTENTION.at(s, 1):
                            wait_for(act, shift_ps, t, per=2, part=b)
                            wait_for(act, p_ps, t, back=2, per=2)
                            nc.scalar.activation(ex[:, t.buf(2), b, :], psS[b][:, :], ACT.Exp, scale=SCALE).then_inc(exp_done, 1)

                    if t := ATTENTION.at(s, -2):
                        wait_for(act, z_ps, t)
                        wait_for(act, lg_ps, t, back=2)
                        nc.scalar.copy(zTs[:, t.buf(2), :], psG[:, P:2 * P]).then_inc(z_sb, 1)
                    if t := ATTENTION.at(s, -1):
                        wait_for(act, oT_ps, t)
                        wait_for(act, attn_ps, t, back=2)
                        nc.scalar.copy(oT[:, t.buf(2), :], psO[:, 384:512]).then_inc(oT_sb, 1)
                    if t := ATTENTION.at(s, -2):
                        nc.scalar.copy(zp[:, t.buf(4), 1, 0:D], zp[:, t.buf(4), 0, 0:D]).then_inc(z2_done, 1)
                    if t := ATTENTION.at(s, 2):
                        wait_for(act, kvr_done, t)
                        wait_for(act, pv_ps, t, back=4)
                        for b in range(2):
                            for c in range(2):
                                src = kvr[b * S:(b + 1) * S, t.buf(2), D:2 * D] \
                                    .rearrange("p (g c r w) -> p g c r w", g=2, c=2, w=DH)[:, :, c, :, :]
                                dst = v9[c * S:(c + 1) * S, t.buf(4), b, 0:PAIRS * VW] \
                                    .rearrange("p (g r c w) -> p g r c w", g=2, c=2, w=DH + 1)[:, :, :, c, 0:DH]
                                nc.scalar.copy(dst, src).then_inc(v9_done, 1)
                    if t := ATTENTION.at(s, 0):
                        for b in range(2):
                            wait_for(act, p_ps, t, per=2, part=b)
                            wait_for(act, pv_ps, t, back=2)
                            nc.scalar.copy(pT[:, t.buf(2), b, :], psP[b][:, :]).then_inc(p_sb, 1)
                    exponentials(0)
                    if t := ATTENTION.at(s, 3):
                        wait_for(act, xc_ps, t)
                        wait_for(act, kv_ps, t, back=2)
                        nc.scalar.copy(xcT[:, t.buf(2), :], psX[:, 0:2 * P]).then_inc(xc_sb, 1)
                    if t := ATTENTION.at(s, 2):
                        wait_for(act, kT_ps, t)
                        wait_for(act, s_ps, t, back=2, per=2)
                        for g in range(4):
                            r = slice(32 * g, 32 * g + 32)
                            last = nc.scalar.copy(kfull[r, t.buf(2), g, :], psK[r, 256:384])
                        last.then_inc(kT_sb, 1)
                    exponentials(1)
                    if (t := ATTENTION.at(s, -2)) and t.buf(2):
                        wait_for(act, gap_done, t)
                        wait_for(act, weight_done, t, back=4)
                        nc.scalar.activation(egap[:, t.buf(4) // 2, :], gap[:, t.buf(4) // 2, :], ACT.Exp).then_inc(egap_done, 2)

                ATTENTION.run(act, attention_step)

                nc.scalar.activation(warm[:, :], tg[:, 0:1], ACT.Silu).then_inc(warm_done, 1)
                act.wait_ge(table_step, 2)
                for e in range(1, E, 2):
                    pad_list(act, e)

                def experts_step(s):
                    if t := EXPERTS.at(s, 1):
                        wait_for(act, a_ps, t)
                        wait_for(act, h_done, t, back=2)
                        nc.scalar.activation(hs[:, t.buf(2), :], psA[t.buf(2)][:, :], ACT.Silu).then_inc(silu_done, 1)
                    if t := EXPERTS.at(s, 0):
                        wait_for(act, y_ps, t)
                        wait_slot(act, y_out, t, 32, back=8)
                        for h in range(2):
                            last = nc.scalar.activation(ys[:, t.buf(8), h, :], psY[t.buf(2)][:, h * D:(h + 1) * D], ACT.Copy,
                                                        scale=zin[:, t.buf(8), h, D + 1:D + 2])
                        last.then_inc(y_sb, 1)

                EXPERTS.run(act, experts_step)

                def combine_step(s):
                    if t := COMBINE.at(s, 0):
                        wait_for(act, total_done, t)
                        act.dma_start(o_c[:, bass.ds(t.val, 1), :, :].squeeze(1), xr_c[:, bass.ds(t.val, 1), :, :].squeeze(1)).then_inc(out_done, 16)

                COMBINE.run(act, combine_step)
                act.wait_ge(out_done, 16 * (NT // CHUNK))

            @block.vector
            def _(dve):
                nc.vector.memset(kfull[:, :, :, :], 0.0).then_inc(zero_ready, 1)
                nc.vector.memset(v9[:, :, :, :], 0.0).then_inc(zero_ready, 1)
                nc.vector.memset(gatew[:, :], 0.0).then_inc(zero_ready, 1)
                nc.vector.memset(mhalf[:, :], -0.5).then_inc(zero_ready, 1)
                dve.wait_ge(zero_ready, 4)
                ones = v9[:, :, :, 0:PAIRS * VW].rearrange("p u b (n w) -> p (u b) n w", w=VW)
                nc.vector.memset(ones[0:S, :, :, DH], 1.0)
                nc.vector.memset(ones[S:P, :, :, VW - 1], 1.0).then_inc(ones_ready, 1)
                dve.wait_ge(weights_in, 16 * 11)
                for g in range(2):
                    nc.vector.tensor_copy(wperm[:, g * 64:(g + 1) * 64].rearrange("p (r c w) -> p r c w", r=4, c=2),
                                          wnat[:, 3, g * 64:(g + 1) * 64].rearrange("p (c r w) -> p r c w", r=4, c=2)).then_inc(wp_ready, 1)
                dve.wait_ge(tanh_ready, 1)
                nc.vector.tensor_scalar(bpg[:, :], bp[:, :], tg[:, 0:1], None, ALU.mult).then_inc(bias_ready, 1)
                dve.wait_ge(ident_ready, 2)
                nc.vector.tensor_scalar(minus[:, :], ident[:, :], -1.0, None, ALU.mult).then_inc(minus_ready, 1)
                dve.wait_ge(route_ready, 5)

                def attention_step(s):
                    pair = t if (t := ATTENTION.at(s, -3)) and t.buf(2) else None
                    if t := pair:
                        q, r = t.buf(4) // 2, slice(t.buf(4) - 1, t.buf(4) + 1)
                        wait_for(dve, place_ps, t)
                        nc.vector.tensor_tensor(place[:, :, :], psG[:, 384:384 + 2 * E].rearrange("p (u e) -> p u e", u=2),
                                                base[:, :].unsqueeze(1).broadcast_to([P, 2, E]), ALU.add).then_inc(place_done, 2)
                        wait_for(dve, egap_done, t)
                        nc.vector.tensor_scalar(den2[:, :], egap[:, q, :], 1.0, None, ALU.add).then_inc(den2_done, 2)
                    if t := ATTENTION.at(s, 2):
                        wait_for(dve, kv_ps, t)
                        wait_for(dve, kvr_done, t, back=2)
                        kv = psK[:, 0:2 * D].rearrange("p (a f) -> p a f", a=2)
                        cs = cosT[:, :].unsqueeze(1).broadcast_to([P, 2, D])
                        nc.vector.tensor_tensor(ropA[:, t.buf(2), :].rearrange("p (a f) -> p a f", a=2), kv, cs, ALU.mult)
                        swapped = psK[:, 0:2 * D].rearrange("p (a f o) -> p a f o", a=2, o=2)[:, :, :, ::-1]
                        sn = sinT[:, :].rearrange("p (f o) -> p f o", o=2).unsqueeze(1).broadcast_to([P, 2, D // 2, 2])
                        nc.vector.tensor_tensor(ropB[:, t.buf(2), :].rearrange("p (a f o) -> p a f o", a=2, o=2),
                                                swapped, sn, ALU.mult).then_inc(rope_done, 1)
                    if t := pair:
                        wait_for(dve, place_done, t)
                        nc.vector.tensor_tensor(hit[:, :, :, :], oh[:, q, :, :, :],
                                                place[:, :, :].unsqueeze(2).broadcast_to([P, 2, 2, E]), ALU.mult).then_inc(hit_done, 2)
                        wait_for(dve, den2_done, t)
                        nc.vector.reciprocal(rden2[:, :], den2[:, :]).then_inc(rden2_done, 2)
                    if t := ATTENTION.at(s, 2):
                        wait_for(dve, q_ps, t)
                        wait_for(dve, s_ps, t, back=2, per=2)
                        nc.vector.tensor_tensor(qblk[:, t.buf(2), :, :, :],
                                                psX[:, 2 * P:3 * P].rearrange("p (b q) -> p b q", b=2).unsqueeze(2).broadcast_to([P, 2, 4, S]),
                                                hmask[:, :].unsqueeze(1).unsqueeze(3).broadcast_to([P, 2, 4, S]),
                                                ALU.mult).then_inc(q_sb, 1)
                    if t := ATTENTION.at(s, 3):
                        wait_for(dve, rs1_done, t)
                        wait_for(dve, xc_ps, t, back=2)
                        nc.vector.tensor_scalar(xn[:, t.buf(2), :], one(xres, t), mv1[:, t.buf(4), 0:1],
                                                rs1[:, t.buf(4):t.buf(4) + 1], ALU.subtract, ALU.mult).then_inc(xn_done, 1)
                    if t := pair:
                        wait_for(dve, hit_done, t)
                        for i in (1, 0):
                            wait_slot(dve, row_out, t + -i, 32, back=4)
                        with nc.allow_low_precision(reason="a row's number: whole and below 2**24"):
                            nc.vector.tensor_reduce(dest[:, q, :, :], hit[:, :, :, :], AX_X, ALU.add).then_inc(dest_done, 2)
                        wait_for(dve, rden2_done, t)
                        nc.vector.tensor_scalar(zp[:, r, 0, D + 1], rden2[:, :], tg[:, 1:2], None, ALU.mult).then_inc(weight_done, 1)
                        nc.vector.scalar_tensor_tensor(out=zp[:, r, 1, D + 1], in0=rden2[:, :], scalar=tg[:, 1:2],
                                                       in1=egap[:, q, :], op0=ALU.mult, op1=ALU.mult).then_inc(weight_done, 1)

                    def maxima(b):
                        if t := ATTENTION.at(s, 1):
                            wait_for(dve, s_ps, t, per=2, part=b)
                            wait_for(dve, shift_ps, t, back=1, per=2, part=b)
                            nc.vector.tensor_reduce(mx[:, b, :], psS[b][:, :].rearrange("p (n k) -> p n k", k=S),
                                                    AX_X, ALU.max).then_inc(mx_done, 1)

                    maxima(0)
                    if (u := ATTENTION.at(s, 4)) and not u.buf(2):
                        wait_for(dve, tiles_in, u + 1, per=32)
                        wait_for(dve, mv1_done, u, back=1)
                        for t in (u, u + 1):
                            carry(dve)
                            nc.vector.bn_stats(st1[:, t.buf(2), :], one(xres, t)).then_inc(st1_done, 1)
                    maxima(1)
                    if t := ATTENTION.at(s, -1):
                        wait_for(dve, attn_ps, t)
                        wait_for(dve, xb_done, t)
                        nc.vector.tensor_tensor(one(xres, t), psG[:, 0:D], one(xres, t), ALU.add).then_inc(x1_done, 1)
                    if t := ATTENTION.at(s, -2):
                        wait_for(dve, lg_ps, t)
                        carry(dve)
                        nc.vector.max(top[:, t.buf(4), :], psG[:, 256:256 + E]).then_inc(top_done, 1)
                    if t := ATTENTION.at(s, -1):
                        wait_for(dve, x1_done, t)
                        carry(dve)
                        nc.vector.bn_stats(st2[:, t.buf(2), :], one(xres, t)).then_inc(st2_done, 1)
                    if t := ATTENTION.at(s, -2):
                        wait_for(dve, top_done, t)
                        carry(dve)
                        nc.vector.max_index(idx[:, t.buf(4), :], top[:, t.buf(4), :], psG[:, 256:256 + E]).then_inc(lg_sb, 1)
                    if t := ATTENTION.at(s, -1):
                        wait_for(dve, st2_done, t)
                        carry(dve)
                        nc.vector.bn_aggr(mv2[:, t.buf(2), :], st2[:, t.buf(2), :]).then_inc(mv2_done, 1)
                    if (u := ATTENTION.at(s, 4)) and not u.buf(2):
                        for t in (u, u + 1):
                            wait_for(dve, st1_done, t)
                            carry(dve)
                            nc.vector.bn_aggr(mv1[:, t.buf(4), :], st1[:, t.buf(2), :]).then_inc(mv1_done, 1)
                    choice = t if (t := ATTENTION.at(s, -2)) and t.buf(2) else None
                    if t := choice:
                        q, r = t.buf(4) // 2, slice(t.buf(4) - 1, t.buf(4) + 1)
                        wait_for(dve, lg_sb, t)
                        nc.vector.tensor_copy(idf[:, q, :, :], idx[:, r, 0:2]).then_inc(idf_done, 2)
                        wait_for(dve, egap_done, t, back=4)
                        nc.vector.tensor_tensor(gap[:, q, :], top[:, r, 1], top[:, r, 0], ALU.subtract).then_inc(gap_done, 2)
                    if t := choice:
                        wait_for(dve, idf_done, t)
                        nc.vector.tensor_tensor(oh[:, q, :, :, :], iot[:, :].unsqueeze(1).unsqueeze(1).broadcast_to([P, 2, 2, E]),
                                                idf[:, q, :, :].unsqueeze(3).broadcast_to([P, 2, 2, E]), ALU.is_equal).then_inc(oh_done, 2)
                    if t := choice:
                        wait_for(dve, oh_done, t)
                        wait_for(dve, place_ps, t, back=4)
                        nc.vector.tensor_tensor(chosen[:, q, :, :], oh[:, q, :, 0, :], oh[:, q, :, 1, :], ALU.add).then_inc(chosen_done, 2)
                    if t := ATTENTION.at(s, -1):
                        wait_for(dve, rs2_done, t)
                        wait_slot(dve, row_out, t, 32, back=4)
                        nc.vector.tensor_scalar(zp[:, t.buf(4), 0, 0:D], one(xres, t), mv2[:, t.buf(2), 0:1],
                                                rs2[:, t.buf(2), :], ALU.subtract, ALU.mult).then_inc(zn_done, 1)
                    if t := ATTENTION.at(s, 0):
                        wait_for(dve, pv_ps, t)
                        wait_for(dve, oT_ps, t, back=2)
                        o = psO[0:S, 0:2 * OROW].rearrange("p (b c) -> p b c", b=2)[:, :, 0:PAIRS * VW] \
                            .rearrange("p b (h w) -> p b h w", w=DH + 1)
                        nc.vector.reciprocal(rden[:, :, :], o[:, :, :, DH]).then_inc(rden_done, 1)
                        wait_for(dve, rden_done, t)
                        for b in range(2):
                            nc.vector.tensor_tensor(on[b * S:(b + 1) * S, t.buf(2), :].rearrange("p (h w) -> p h w", w=DH),
                                                    o[:, b, :, 0:DH],
                                                    rden[:, b, :].unsqueeze(2).broadcast_to([S, H, DH]),
                                                    ALU.mult).then_inc(on_done, 1)

                ATTENTION.run(dve, attention_step)

                dve.wait_ge(count_ps, 1)
                nc.vector.tensor_copy(cnt[:, :], psG[:, 0:E]).then_inc(table_step, 1)
                dve.wait_ge(table_step, 1)
                nc.vector.tensor_tensor(padrow[:, :], cnt[:, :], base[:, :], ALU.add).then_inc(table_step, 1)
                dve.wait_ge(table_step, 2)
                nc.vector.tensor_scalar(ntu[:, 0, :], cnt[:, :], float(ET - 1), None, ALU.add).then_inc(table_step, 1)
                dve.wait_ge(table_step, 3)
                nc.vector.tensor_scalar(ntu[:, 1, :], ntu[:, 0, :], ET.bit_length() - 1, None, ALU.logical_shift_right).then_inc(table_step, 1)
                dve.wait_ge(table_step, 4)
                nc.vector.tensor_copy(ntf[:, :], ntu[:, 1, :]).then_inc(table_step, 1)
                dve.wait_ge(table_step, 5)
                nc.vector.tensor_scalar(jump[:, :], ntf[:, :], -float(ET), float(CAP), ALU.mult, ALU.add).then_inc(table_step, 1)
                dve.wait_ge(table_step, 6)
                nc.vector.tensor_tensor_scan(upto[:, :], ntf[:, :], zero8[:, :], 0.0, ALU.add, ALU.add).then_inc(table_step, 1)
                dve.wait_ge(table_step, 7)
                nc.vector.tensor_tensor(past[:, :, :], upto[:, :].unsqueeze(1).broadcast_to([P, NET, E]),
                                        tile_no[:, :].unsqueeze(2).broadcast_to([P, NET, E]), ALU.is_le).then_inc(table_step, 1)
                dve.wait_ge(table_step, 8)
                nc.vector.tensor_reduce(tfl[:, 0, :], past[:, :, :], AX_X, ALU.add)
                nc.vector.tensor_tensor(hop[:, :, :], past[:, :, :], jump[:, :].unsqueeze(1).broadcast_to([P, NET, E]), ALU.mult).then_inc(table_step, 1)
                dve.wait_ge(table_step, 9)
                nc.vector.tensor_reduce(tfl[:, 1, :], hop[:, :, :], AX_X, ALU.add).then_inc(table_step, 1)
                dve.wait_ge(table_step, 10)
                nc.vector.tensor_scalar(table[:, 0, :], tfl[:, 0, :], float(E - 1), None, ALU.min).then_inc(table_step, 1)
                dve.wait_ge(table_step, 11)
                nc.vector.tensor_tensor(table[:, 1, :], tfl[:, 1, :], first_row[:, :], ALU.add).then_inc(table_step, 1)
                dve.wait_ge(table_step, 12)

                dve.wait_ge(experts_in, 16 * (2 + E))

                def experts_step(s):
                    if t := EXPERTS.at(s, 2):
                        e = expert(dve, t)
                        wait_for(dve, b_ps, t, back=2)
                        nc.vector.tensor_copy(wcur[:, t.buf(2), :, :], w01[:, bass.ds(e, 1), :, :].squeeze(1)).then_inc(w_done, 1)
                        wait_for(dve, ez_ps, t)
                        nc.vector.tensor_copy(zT[:, t.buf(2), :], psZ[t.buf(2)][:, 0:ET]).then_inc(ez_sb, 1)
                    if t := EXPERTS.at(s, 1):
                        wait_for(dve, b_ps, t)
                        wait_for(dve, silu_done, t)
                        wait_for(dve, y_ps, t, back=2)
                        nc.vector.tensor_tensor(hm[:, t.buf(2), :, :].rearrange("p k t -> p (k t)"), psB[t.buf(2)][:, :], hs[:, t.buf(2), :],
                                                ALU.mult).then_inc(h_done, 1)

                EXPERTS.run(dve, experts_step)

                def combine_step(s):
                    if t := COMBINE.at(s, 0):
                        wait_slot(dve, y_in, t, 16)
                        ya, yb = yy[:, t.buf(4), :, 0, :], yy[:, t.buf(4), :, 1, :]
                        nc.vector.tensor_tensor(ya, ya, yb, ALU.add).then_inc(sum_done, 1)
                        wait_for(dve, sum_done, t)
                        x1 = xr_c[:, bass.ds(t.val, 1), :, :].squeeze(1)
                        nc.vector.tensor_tensor(x1, x1, ya, ALU.add).then_inc(total_done, 1)

                COMBINE.run(dve, combine_step)

            @block.gpsimd
            def _(pool):
                nc.gpsimd.memset(ident[:, :], 0.0).then_inc(ident_ready, 1)
                pool.wait_ge(ident_ready, 1)
                nc.gpsimd.affine_select(out=ident[:, :], in_=ident[:, :], compare_op=ALU.not_equal, fill=1.0, base=0,
                                        pattern=[[-1, P]], channel_multiplier=1).then_inc(ident_ready, 1)
                nc.gpsimd.memset(allone[:, :], 1.0).then_inc(route_ready, 1)
                nc.gpsimd.memset(before[:, :, :, :], 0.0).then_inc(route_ready, 1)
                pool.wait_ge(route_ready, 2)
                pool.wait_ge(zero_ready, 4)
                pool.wait_ge(ones_ready, 1)
                pool.wait_ge(bias_ready, 1)

                nc.gpsimd.iota(iot[:, :], pattern=[[1, E]], base=0, channel_multiplier=0,
                               allow_small_or_imprecise_dtypes=True).then_inc(route_ready, 1)
                nc.gpsimd.iota(base[:, :], pattern=[[CAP, E]], base=0, channel_multiplier=0,
                               allow_small_or_imprecise_dtypes=True).then_inc(route_ready, 1)
                nc.gpsimd.iota(tokid[:, :, :], pattern=[[2 * P, NT], [1, 2]], base=0, channel_multiplier=2).then_inc(pad_ready, 1)
                nc.gpsimd.affine_select(out=lower[:, :], in_=allone[:, :], compare_op=ALU.is_gt, fill=0.0, base=0,
                                        pattern=[[1, P]], channel_multiplier=-1).then_inc(route_ready, 1)
                pool.wait_ge(pad_ready, 1)

                nc.gpsimd.iota(tile_no[:, :], pattern=[[1, NET]], base=0, channel_multiplier=0,
                               allow_small_or_imprecise_dtypes=True).then_inc(e_const, 1)
                nc.gpsimd.iota(first_row[:, :], pattern=[[ET, NET]], base=0, channel_multiplier=0,
                               allow_small_or_imprecise_dtypes=True).then_inc(e_const, 1)
                nc.gpsimd.memset(zero8[:, :], 0.0).then_inc(e_const, 1)
                nc.gpsimd.memset(pad[:, :, :], 0.0).then_inc(e_const, 1)
                pool.wait_ge(e_const, 4)
                nc.gpsimd.iota(pad[:, :, D:D + 1].bitcast(U32), pattern=[[0, 2], [0, 1]], base=NOWHERE, channel_multiplier=0).then_inc(e_const, 1)

                def attention_step(s):
                    if t := ATTENTION.at(s, 2):
                        wait_for(pool, rope_done, t)
                        wait_for(pool, kT_ps, t, back=2)
                        wait_for(pool, v9_done, t, back=2, per=4)
                        nc.gpsimd.tensor_tensor(kvr[:, t.buf(2), :], ropA[:, t.buf(2), :], ropB[:, t.buf(2), :],
                                                ALU.add).then_inc(kvr_done, 1)
                    if (t := ATTENTION.at(s, -3)) and t.buf(2):
                        r = slice(t.buf(4) - 1, t.buf(4) + 1)
                        src = tokid[:, t.val - 1:t.val + 1, :] if isinstance(t.val, int) else tokid[:, bass.ds(t.val - 1, 2), :]
                        for i in (1, 0):
                            wait_slot(pool, row_out, t + -i, 32, back=4)
                        carry(pool)
                        nc.gpsimd.tensor_copy(zp[:, r, :, D].bitcast(U32), src).then_inc(tok_done, 2)
                    if t := ATTENTION.at(s, -4):
                        pair = t + (0 if t.buf(2) else 1)
                        wait_for(pool, dest_done, pair)
                        wait_for(pool, weight_done, pair)
                        wait_for(pool, tok_done, pair)
                        wait_for(pool, z2_done, t)
                        carry(pool)
                        for j in range(2):
                            nc.gpsimd.indirect_dma_start(
                                lists, bass.IndirectOffsetOnAxis(ap=dest[:, t.buf(4) // 2, t.buf(2), j:j + 1], axis=0),
                                zp[:, t.buf(4), j, :], None).then_inc(row_out[t.buf(4)], 16)
                    if t := ATTENTION.at(s, -1):
                        wait_for(pool, mv2_done, t)
                        carry(pool)
                        nc.gpsimd.tensor_scalar(ve2[:, t.buf(2), :], mv2[:, t.buf(2), 1:2], EPS, None, ALU.add).then_inc(ve2_done, 1)
                        wait_for(pool, ve2_done, t)
                        wait_for(pool, zn_done, t, back=2)
                        nc.gpsimd.tensor_tensor(rs2[:, t.buf(2), :], ve2[:, t.buf(2), :], mhalf[:, 0:1], ALU.pow).then_inc(rs2_done, 1)
                    if (t := ATTENTION.at(s, 4)) and not t.buf(2):
                        r = slice(t.buf(4), t.buf(4) + 2)
                        wait_for(pool, mv1_done, t + 1)
                        wait_for(pool, xn_done, t, back=3)
                        carry(pool)
                        nc.gpsimd.tensor_scalar(ve1[:, r], mv1[:, r, 1], EPS, None, ALU.add).then_inc(ve1_done, 2)
                        wait_for(pool, ve1_done, t + 1)
                        nc.gpsimd.tensor_tensor(rs1[:, r], ve1[:, r], mhalf[:, :], ALU.pow).then_inc(rs1_done, 2)
                    if t := ATTENTION.at(s, 3):
                        wait_for(pool, xn_done, t)
                        nc.gpsimd.tensor_tensor(one(xres, t), one(xres, t), bpg[:, :], ALU.add).then_inc(xb_done, 1)
                    if (t := ATTENTION.at(s, -2)) and t.buf(2):
                        q = t.buf(4) // 2
                        wait_for(pool, chosen_done, t)
                        wait_for(pool, before_done, t, back=2)
                        nc.gpsimd.tensor_tensor(before[:, q, 1, :], before[:, q, 0, :], chosen[:, q, 0, :], ALU.add).then_inc(before_done, 1)
                        wait_for(pool, before_done, t, back=1)
                        wait_for(pool, place_ps, t, back=2)
                        nc.gpsimd.tensor_tensor(before[:, 1 - q, 0, :], before[:, q, 1, :], chosen[:, q, 1, :], ALU.add).then_inc(before_done, 1)

                ATTENTION.run(pool, attention_step)

                def experts_step(s):
                    if t := EXPERTS.at(s, -1):
                        wait_for(pool, y_sb, t)
                        carry(pool)
                        for h in range(2):
                            nc.gpsimd.indirect_dma_start(
                                results, bass.IndirectOffsetOnAxis(ap=zin[:, t.buf(8), h, D:D + 1].bitcast(U32), axis=0),
                                ys[:, t.buf(8), h, :], None, bounds_check=NOWHERE - 1, oob_is_err=False).then_inc(y_out[t.buf(8)], 16)

                EXPERTS.run(pool, experts_step)


_INS = ["x", "ctx_1024", "g_xattn", "g_ffn", "L0_xattn_Wq", "L0_xattn_Wk", "L0_xattn_Wv", "L0_xattn_Wp", "L0_xattn_bp",
        "L0_ffn_gate_kernel", "L0_ffn_w0_kernel", "L0_ffn_w1_kernel", "L0_ffn_wo_kernel"]


def shape_constants():
    import numpy as np
    theta = (np.float32(1.0) / np.float32(10000.0) ** (np.float32(2.0) * np.arange(D // 2, dtype=np.float32) / np.float32(D))).astype(np.float32)
    ang = np.arange(S, dtype=np.float32)[:, None] * theta[None, :]
    cos, sin = np.cos(ang), np.sin(ang)
    cos2 = np.repeat(cos, 2, axis=1)
    sin2 = np.stack([-sin, sin], axis=-1).reshape(S, D)
    mask = (np.arange(D)[:, None] // DH % 4 == np.arange(4)[None, :])
    return {"rope_cos": np.tile(cos2, (P // S, 1)).astype(np.float32), "rope_sin": np.tile(sin2, (P // S, 1)).astype(np.float32),
            "head_mask": mask.astype(np.float32)}


def kernel(**inputs):
    import numpy as _np
    import concourse.bacc as _bacc
    from concourse import mybir as _mybir
    from concourse.bass_utils import run_bass_kernel_spmd as _run

    nc = _bacc.Bacc("TRN2", target_bir_lowering=False, num_devices=1)
    arrays, args = {}, {}
    for name, a in [(n, inputs[n]) for n in _INS] + list(shape_constants().items()):
        a = _np.ascontiguousarray(a)
        arrays[f"in_{name}_dram"] = a
        args[name] = nc.dram_tensor(f"in_{name}_dram", a.shape, _mybir.dt.from_np(a.dtype), kind="ExternalInput").ap()
    args["lists"] = nc.dram_tensor("lists", (ZROWS, ROW), F32, kind="Internal").ap()
    args["results"] = nc.dram_tensor("results", (2 * NT * P, D), F32, kind="Internal").ap()
    out = nc.dram_tensor("out_0_dram", (NB, S, D), F32, kind="ExternalOutput").ap()
    flamingo_block(nc, args, out)
    r = _run(nc, [arrays], core_ids=[0])
    return r.results[0]["out_0_dram"]
```
